# Optimizing a Trainium2 kernel written in Bass

```python
import numpy as np
import jax
import jax.numpy as jnp

def _softmax(x, axis=-1):
    return jax.nn.softmax(x, axis=axis)

def _gelu(x):
    return jax.nn.gelu(x, approximate=True)

def _silu(x):
    return jax.nn.silu(x)

def _sigmoid(x):
    return jax.nn.sigmoid(x)

def _layernorm(x, axis=-1, eps=1e-05):
    m = jnp.mean(x, axis=axis, keepdims=True)
    v = jnp.var(x, axis=axis, keepdims=True)
    return (x - m) / jnp.sqrt(v + eps)

def _scatter_add(tgt, idx, src, axis=0):
    return tgt.at[idx].add(src)

def _segment_sum(src, seg, n):
    return jax.ops.segment_sum(src, seg, n)
kernel_name = 'mk_adj_resnorm_d2_adj_r2_21b5a4'

def setup_inputs(seed: int=0):
    np.random.seed(seed)
    _w = jnp.asarray

    def _rec_inputs():
        import jax
        import jax.numpy as jnp
        _gk = jax.random.key(seed)
        x = -0.0005207 + 1.001 * jax.random.normal(jax.random.fold_in(_gk, 1), (4096, 128), jnp.float32)
        _a = jax.random.bernoulli(jax.random.fold_in(_gk, 2), 0.00390625, (4096, 4096))
        _a = jnp.logical_or(_a, jnp.swapaxes(_a, -1, -2))
        _a = jnp.logical_or(_a, jnp.eye(4096, dtype=bool))
        adj = _a.astype(jnp.int32)
        return (x, adj)
    x, adj = _rec_inputs()

    def _L0_gnn_setup():
        import jax, jax.numpy as jnp
        import numpy as np
        N, IN_DIM, OUT_DIM = (4096, 128, 128)
        NEG_INF = -1000000000.0
        key = jax.random.key(seed)
        k1, k2, k3, k4 = jax.random.split(key, 4)
        X = jax.random.normal(k1, (N, IN_DIM), dtype=jnp.float32)
        A = jax.random.randint(k2, (N, N), 0, 2).astype(jnp.int32)
        W_fc = jax.random.normal(k3, (IN_DIM, OUT_DIM), dtype=jnp.float32) * (1.0 / np.sqrt(IN_DIM))
        b_fc = jnp.zeros((OUT_DIM,), dtype=jnp.float32)
        w_att = jax.random.normal(k4, (2 * OUT_DIM,), dtype=jnp.float32) * (1.0 / np.sqrt(2 * OUT_DIM))
        b_att = jnp.zeros((), dtype=jnp.float32)
        return {'X': X, 'A': A, 'W_fc': W_fc, 'b_fc': b_fc, 'w_att': w_att, 'b_att': b_att}
    _L0_gnn_all = _L0_gnn_setup()
    _L0_gnn_in = {k: v for k, v in _L0_gnn_all.items() if k in ('W_fc', 'b_fc', 'w_att', 'b_att')}
    del _L0_gnn_all

    def _L1_gnn_setup():
        import jax, jax.numpy as jnp
        import numpy as np
        N = 4096
        D = 128
        NEG_SLOPE = 0.01
        MASK_VAL = -1000000000000.0
        key = jax.random.key(seed)
        k1, k2, k3, k4 = jax.random.split(key, 4)
        x = jax.random.normal(k1, (N, D), dtype=jnp.float32)
        adj = jax.random.randint(k2, (N, N), 0, 2, dtype=jnp.int32)
        W = jax.random.normal(k3, (D, D), dtype=jnp.float32) * (1.0 / np.sqrt(D))
        a = jax.random.normal(k4, (2 * D, 1), dtype=jnp.float32) * (1.0 / np.sqrt(2 * D))
        return {'x': x, 'adj': adj, 'W': W, 'a': a}
    _L1_gnn_all = _L1_gnn_setup()
    _L1_gnn_in = {k: v for k, v in _L1_gnn_all.items() if k in ('W', 'a')}
    del _L1_gnn_all
    return {'x': x, 'adj': adj, 'L0_gnn_W_fc': _L0_gnn_in['W_fc'], 'L0_gnn_b_fc': _L0_gnn_in['b_fc'], 'L0_gnn_w_att': _L0_gnn_in['w_att'], 'L0_gnn_b_att': _L0_gnn_in['b_att'], 'L1_gnn_W': _L1_gnn_in['W'], 'L1_gnn_a': _L1_gnn_in['a']}

def reference(x, adj, L0_gnn_W_fc, L0_gnn_b_fc, L0_gnn_w_att, L0_gnn_b_att, L1_gnn_W, L1_gnn_a):
    import jax
    import jax.numpy as jnp

    def _L0_gnn_ref(X, A, W_fc, b_fc, w_att, b_att):
        import jax, jax.numpy as jnp
        import numpy as np
        N, IN_DIM, OUT_DIM = (4096, 128, 128)
        NEG_INF = -1000000000.0
        H = X @ W_fc + b_fc
        d = H.shape[1]
        s_src = H @ w_att[:d]
        s_dst = H @ w_att[d:]
        scores = s_src[:, None] + s_dst[None, :] + b_att
        scores = jnp.where(A > 0, scores, jnp.float32(NEG_INF))
        alpha = jax.nn.softmax(scores, axis=1)
        return alpha @ H

    def _L1_gnn_ref(x, adj, W, a):
        import jax, jax.numpy as jnp
        import numpy as np
        N = 4096
        D = 128
        NEG_SLOPE = 0.01
        MASK_VAL = -1000000000000.0
        h = x @ W
        e_src = h @ a[:D, 0]
        e_dst = h @ a[D:, 0]
        e = e_src[:, None] + e_dst[None, :]
        e = jnp.where(e > 0, e, NEG_SLOPE * e)
        att_logits = jnp.where(adj > 0, e, MASK_VAL)
        attention = jax.nn.softmax(att_logits, axis=1)
        h_prime = attention @ h
        return jax.nn.elu(h_prime)
    x = _layernorm(x + _L0_gnn_ref(x, adj, L0_gnn_W_fc, L0_gnn_b_fc, L0_gnn_w_att, L0_gnn_b_att), axis=-1)
    x = _layernorm(x + _L1_gnn_ref(x, adj, L1_gnn_W, L1_gnn_a), axis=-1)
    return x

_drawn_inputs = setup_inputs


def setup_inputs(seed=0):
    import zlib

    import numpy as np

    out = dict(_drawn_inputs(seed))
    spreads = {'L0_gnn_b_fc': (0.0, 0.1)}
    factors = {}
    for name, (base, spread) in spreads.items():
        noise = np.random.default_rng([zlib.crc32(name.encode()), seed]).standard_normal(out[name].shape)
        drawn = base * np.exp(spread * noise) if base else spread * noise
        out[name] = jnp.asarray(drawn.astype(out[name].dtype))
    for name, factor in factors.items():
        out[name] = (out[name] * factor).astype(out[name].dtype)
    return out
```

```python
from contextlib import ExitStack

import concourse.bass as bass
from concourse import mybir

F32 = mybir.dt.float32
BF16 = mybir.dt.bfloat16
FP8 = mybir.dt.float8e4
U8 = mybir.dt.uint8
U16 = mybir.dt.uint16
I32 = mybir.dt.int32
ALU = mybir.AluOpType
ACT = mybir.ActivationFunctionType
AX = mybir.AxisListType

P = 128
N = 4096
D = 128
TILES = N // P
PAIRS = TILES // 2
CHUNKS = 4
CW = N // CHUNKS
PARTS = 3
GROUP = 4
GROUPS = TILES // GROUP
BANK = 512
MASK_BYTE = 64
LIMIT = 30.0
TINY = 1e-30
EMPTY = 1e-20
EPS = 1e-5


def views(x, adj, out):
    return (x.rearrange("(q k b) f -> k q (b f)", k=P, b=2),
            adj.rearrange("(q k b) j -> q b k j", k=P, b=2),
            out.rearrange("(q k b) f -> k q (b f)", k=P, b=2))


def layer_one(nc, keep, x_rows, adj_rows, w_fc, b_fc, w_att, b_att, w_gat, a_gat):
    store, x_sb, sd1, lsum, sd0, w_out, ident = (keep[n] for n in (
        "store", "x_sb", "sd1", "lsum", "sd0", "w_out", "ident"))
    with ExitStack() as ctx:
        sb = lambda name, shape, dt: ctx.enter_context(nc.sbuf_tensor(name, shape, dt))
        sem = lambda name: ctx.enter_context(nc.semaphore(name))
        parts = sb("parts", [P, TILES, PARTS, D + 1], BF16)
        adj_sb = sb("adj_sb", [P, CHUNKS, CW], I32)
        mask8 = sb("mask8", [P, 2, N], U8)
        stage = sb("stage", [P, 2, N], U8)
        ident16 = sb("ident16", [P, P], BF16)
        att_col = sb("att_col", [P, 2], F32)
        gat_col = sb("gat_col", [P, 2], F32)
        w0sd = sb("w0sd", [P, 2], F32)
        bias_row = sb("bias_row", [P, D], F32)
        avec = sb("avec", [P, 3, D], F32)
        dconst = sb("dconst", [P, 2], F32)
        b_att_sb = sb("b_att_sb", [P, 1], F32)
        e_in = sb("e_in", [P, 2, GROUP], F32)
        eps = sb("eps", [P, 1], F32)
        sums = sb("sums", [P, D + 1], F32)
        linv = sb("linv", [P, 1], F32)
        held_l = sb("held_l", [P, 1], F32)
        y = sb("y", [P, D], F32)
        stats = sb("stats", [P, 6], F32)
        mv = sb("mv", [P, 2], F32)
        std = sb("std", [P, 1], F32)
        rstd = sb("rstd", [P, 1], F32)
        prod = sb("prod", [P, 3, D], F32)
        def late(tile, at, shape):
            n = 1
            for s in shape:
                n *= s
            flat = store[:, tile, :].bitcast(F32)[:, at:at + n]
            if len(shape) == 1:
                return flat
            return flat.rearrange("p (a c) -> p a c", a=shape[0])
        xT = [late(TILES - 1 - s, 0, [GROUP * P]) for s in range(2)]
        g32 = [late(TILES - 3 - s, 0, [GROUP, D + 1]) for s in range(2)]
        wT = late(TILES - 5, 0, [2, P])
        gat_rep = late(TILES - 5, 256, [2, P])
        last_rep = late(TILES - 5, 512, [P])
        att_row = late(TILES - 5, 640, [2, D])
        w0, w1 = late(TILES - 6, 0, [D]), late(TILES - 6, D, [D])

        turned = ctx.enter_context(nc.psum_tensor("turned", [P, 2, PAIRS, P], BF16))
        acc = ctx.enter_context(nc.psum_tensor("acc", [P, 2, BANK], F32))
        hps = ctx.enter_context(nc.psum_tensor("hps", [P, 2, BANK], F32))
        spare = [turned[:, n // 2, :, :].rearrange("p q l -> p (q l)").bitcast(F32)[:, BANK * (n % 2):BANK * (n % 2 + 1)]
                 for n in range(4)]
        wT_ps, w0sd_ps = spare[0][:, 0:256], spare[0][:, 256:258]
        avec_ps, last_ps = spare[2][:, 0:256], spare[2][:, 256:384]
        sd_ps = [spare[2 * s + 1][:, 0:2 * GROUP].rearrange("p (t c) -> p t c", c=2) for s in range(2)]

        x_landed = [sem(f"x_landed{g}") for g in range(4)]
        w_landed, w_small_landed = sem("w_landed"), sem("w_small_landed")
        adj_landed = [sem(f"adj_landed{c}") for c in range(CHUNKS)]
        ident_ready, ident16_ready, consts_ready = sem("ident_ready"), sem("ident16_ready"), sem("consts_ready")
        pool_step = sem("pool_step")
        bias_added = sem("bias_added")
        w_turned, w_copied, reps_ready, w_made = sem("w_turned"), sem("w_copied"), sem("reps_ready"), sem("w_made")
        w0sd_ready = sem("w0sd_ready")
        dconst_ready, prep_step = sem("dconst_ready"), sem("prep_step")
        x_turned, xT_ready, h_ready, e_in_ready, e_ready = (sem(n) for n in (
            "x_turned", "xT_ready", "h_ready", "e_in_ready", "e_ready"))
        g_ready, hi_ready, rest_ready, mid_ready, parts_ready = (sem(n) for n in (
            "g_ready", "hi_ready", "rest_ready", "mid_ready", "parts_ready"))
        chunk_done, mask_turned, staged, stored, sums_ready = (sem(n) for n in (
            "chunk_done", "mask_turned", "staged", "stored", "sums_ready"))
        acc_drained, tile_step, var_ready, std_ready = (sem(n) for n in (
            "acc_drained", "tile_step", "var_ready", "std_ready"))
        STEPS = 7

        block = ctx.enter_context(nc.Block())

        @block.sync
        def _(sp):
            for g in range(4):
                sp.dma_start(x_sb[:, 8 * g:8 * g + 8, :].rearrange("p (q b) f -> p q (b f)", b=2),
                             x_rows[:, 4 * g:4 * g + 4, :]).then_inc(x_landed[g], 16)

            def load(q, first=False):
                for b in range(2):
                    for c in range(CHUNKS):
                        if not (first and b == 0):
                            sp.wait_ge(chunk_done, q * 2 * CHUNKS + (b - 1) * CHUNKS + c + 1)
                        sp.dma_start(adj_sb[:, c, :],
                                     adj_rows[q, b, :, c * CW:(c + 1) * CW]).then_inc(adj_landed[c], 16)

            load(0, first=True)
            with sp.Fori(1, PAIRS) as q:
                load(q)

        @block.gpsimd
        def _(pool):
            nc.gpsimd.memset(ident[:, :], 0.0).then_inc(pool_step, 1)
            pool.wait_ge(pool_step, 1)
            nc.gpsimd.affine_select(out=ident[:, :], in_=ident[:, :], compare_op=ALU.not_equal, fill=1.0,
                                    base=0, pattern=[[-1, P]], channel_multiplier=1).then_inc(ident_ready, 1)
            pool.wait_ge(ident_ready, 1)
            nc.gpsimd.tensor_copy(ident16[:, :], ident[:, :]).then_inc(ident16_ready, 1)
            nc.gpsimd.memset(eps[:, :], EPS).then_inc(consts_ready, 1)
            nc.gpsimd.memset(avec[:, 2, :], 1.0 / D).then_inc(consts_ready, 1)
            pool.wait_ge(w_small_landed, 16 * 5)
            for g in range(GROUPS):
                pool.wait_ge(x_turned, g + 1)
                xg = x_sb[:, GROUP * g:GROUP * (g + 1), :]
                nc.gpsimd.tensor_tensor(xg, xg, bias_row[:, :].rearrange("p (o d) -> p o d", o=1).to_broadcast(
                    [P, GROUP, D]), ALU.add).then_inc(bias_added, 1)

        @block.scalar
        def _(act):
            act.dma_start(w0, w_fc).then_inc(w_landed, 16)
            act.dma_start(w1, w_gat).then_inc(w_landed, 16)
            with nc.allow_non_contiguous_dma(reason="256 single values"):
                act.dma_start(att_col[:, :], w_att.rearrange("(s d) -> d s", s=2)).then_inc(w_small_landed, 16)
                act.dma_start(gat_col[:, :], a_gat.rearrange("(s d) o -> d (s o)", s=2)).then_inc(w_small_landed, 16)
            act.dma_start(bias_row[:, :], b_fc.rearrange("(o d) -> o d", o=1).to_broadcast([P, D])
                          ).then_inc(w_small_landed, 16)
            act.dma_start(b_att_sb[:, :], b_att.to_broadcast([P, 1])).then_inc(w_small_landed, 16)
            act.dma_start(att_row.rearrange("p s d -> p (s d)"),
                          w_att.rearrange("(o d) -> o d", o=1).to_broadcast([P, 2 * D])).then_inc(w_small_landed, 16)
            act.wait_ge(w_turned, 1)
            nc.scalar.copy(wT.rearrange("p a c -> p (a c)"), wT_ps).then_inc(w_copied, 1)
            act.wait_ge(w_made, 1)
            nc.scalar.copy(w0sd[:, :], w0sd_ps).then_inc(w0sd_ready, 1)
            act.wait_ge(dconst_ready, 1)

            def turn_out(g):
                act.wait_ge(x_turned, g + 1)
                if g >= 2:
                    act.wait_ge(h_ready, g - 1)
                nc.scalar.copy(xT[g % 2], acc[:, g % 2, :]).then_inc(xT_ready, 1)

            turn_out(0)
            for g in range(GROUPS):
                if g + 1 < GROUPS:
                    turn_out(g + 1)
                act.wait_ge(e_in_ready, g + 1)
                nc.scalar.activation(g32[g % 2][:, :, D], e_in[:, g % 2, :], ACT.Exp).then_inc(e_ready, 1)
                act.wait_ge(g_ready, g + 1)
                nc.scalar.copy(parts[:, GROUP * g:GROUP * (g + 1), 0, :], g32[g % 2]).then_inc(hi_ready, 1)
                act.wait_ge(rest_ready, g + 1)
                nc.scalar.copy(parts[:, GROUP * g:GROUP * (g + 1), 1, :], g32[g % 2]).then_inc(mid_ready, 1)

            act.wait_ge(consts_ready, 1)

            def stage_mask(t, s, free):
                act.wait_ge(mask_turned, t + 1)
                if free:
                    act.wait_ge(sums_ready, t - 1)
                nc.scalar.copy(stage[:, s, :].bitcast(U16),
                               turned[:, s].rearrange("p q l -> p (q l)").bitcast(U16)).then_inc(staged, 1)

            def store_mask(t, s):
                nc.scalar.copy(store[:, bass.ds(t, 1), :].rearrange("p t n -> p (t n)").bitcast(U16),
                               turned[:, s].rearrange("p q l -> p (q l)").bitcast(U16)).then_inc(stored, 1)

            def root(t):
                act.wait_ge(var_ready, t + 1)
                nc.scalar.activation(std[:, :], mv[:, 1:2], ACT.Sqrt, bias=eps[:, :]).then_inc(std_ready, 1)

            def pair(q, first=False, last=False):
                stage_mask(2 * q + 1, 1, not first)
                if not first:
                    root(2 * q - 1)
                store_mask(2 * q + 1, 1)
                if not last:
                    stage_mask(2 * q + 2, 0, True)
                root(2 * q)
                if not last:
                    store_mask(2 * q + 2, 0)

            stage_mask(0, 0, False)
            store_mask(0, 0)
            pair(0, first=True)
            with act.Fori(1, PAIRS - 1) as q:
                pair(q)
            pair(PAIRS - 1, last=True)
            root(TILES - 1)

        @block.vector
        def _(dve):
            steps = [0]

            def link(ins):
                steps[0] += 1
                ins.then_inc(prep_step, 1)
                dve.wait_ge(prep_step, steps[0])

            dve.wait_ge(w_small_landed, 16 * 5)
            nc.vector.tensor_copy(gat_rep, gat_col[:, :].rearrange("p (s o) -> p s o", o=1).to_broadcast([P, 2, P]))
            dve.wait_ge(ident_ready, 1)
            nc.vector.tensor_copy(last_rep, ident[:, P - 1:P].to_broadcast([P, P])).then_inc(reps_ready, 1)
            link(nc.vector.tensor_tensor(att_row, att_row, bias_row[:, :].rearrange("p (o d) -> p o d", o=1)
                                         .to_broadcast([P, 2, D]), ALU.mult))
            link(nc.vector.tensor_reduce(dconst[:, :], att_row, AX.X, ALU.add))
            nc.vector.tensor_tensor(dconst[:, 0:1], dconst[:, 0:1], b_att_sb[:, :], ALU.add).then_inc(dconst_ready, 1)
            dve.wait_ge(w_made, 1)
            nc.vector.tensor_copy(avec[:, 0:2, :], avec_ps.rearrange("p (s d) -> p s d", s=2))
            nc.vector.tensor_tensor(w_out[:, 0:D], w1, last_ps, ALU.subtract)
            nc.vector.tensor_copy(w_out[:, D:D + 1], ident[:, P - 1:P]).then_inc(consts_ready, 1)

            def convert(t, s, c, free):
                dve.wait_ge(adj_landed[c], 16 * (t + 1))
                if free and c == 0:
                    dve.wait_ge(mask_turned, t - 1)
                nc.vector.tensor_scalar(mask8[:, s, c * CW:(c + 1) * CW], adj_sb[:, c, :], 0.0, float(MASK_BYTE),
                                        ALU.is_gt, ALU.mult).then_inc(chunk_done, 1)

            for g in range(GROUPS):
                gs = slice(GROUP * g, GROUP * (g + 1))
                dve.wait_ge(h_ready, g + 1)
                link(nc.vector.tensor_tensor(sd0[:, gs, :], sd_ps[g % 2], dconst[:, :].rearrange(
                    "p (o c) -> p o c", o=1).to_broadcast([P, GROUP, 2]), ALU.add))
                if g >= 2:
                    dve.wait_ge(e_ready, g - 1)
                nc.vector.tensor_scalar(e_in[:, g % 2, :], sd0[:, gs, 1], LIMIT, -LIMIT, ALU.min, ALU.max
                                        ).then_inc(e_in_ready, 1)
                if g == 5:
                    for c in range(CHUNKS):
                        convert(0, 0, c, False)
                dve.wait_ge(e_ready, g + 1)
                gg = g32[g % 2]
                nc.vector.tensor_tensor(gg[:, :, 0:D], hps[:, g % 2, :].rearrange("p (t d) -> p t d", t=GROUP),
                                        gg[:, :, D:D + 1].to_broadcast([P, GROUP, D]), ALU.mult).then_inc(g_ready, 1)
                dve.wait_ge(hi_ready, g + 1)
                nc.vector.tensor_tensor(gg, gg, parts[:, gs, 0, :], ALU.subtract).then_inc(rest_ready, 1)
                dve.wait_ge(mid_ready, g + 1)
                nc.vector.tensor_tensor(parts[:, gs, 2, :], gg, parts[:, gs, 1, :], ALU.subtract).then_inc(parts_ready, 1)
            for c in range(CHUNKS):
                convert(1, 1, c, False)

            def finish(t, s, cvt):
                def step(ins):
                    n[0] += 1
                    ins.then_inc(tile_step, 1)

                def stepped():
                    dve.wait_ge(tile_step, STEPS * t + n[0])
                n = [0]
                dve.wait_ge(sums_ready, t + 1)
                nc.vector.tensor_reduce(sums[:, :], acc[:, s, 0:PARTS * (D + 1)].rearrange(
                    "p (c f) -> p f c", c=PARTS), AX.X, ALU.add).then_inc(acc_drained, 1)
                cvt(0)
                dve.wait_ge(acc_drained, t + 1)
                step(nc.vector.tensor_scalar(held_l[:, :], sums[:, D:D + 1], TINY, None, ALU.max))
                cvt(1)
                stepped()
                step(nc.vector.reciprocal(linv[:, :], held_l[:, :]))
                nc.vector.tensor_copy(lsum[:, bass.ds(t, 1)], held_l[:, :])
                cvt(2)
                stepped()
                xt = x_sb[:, bass.ds(t, 1), :].rearrange("p o f -> p (o f)")
                step(nc.vector.scalar_tensor_tensor(out=y[:, :], in0=sums[:, 0:D], scalar=linv[:, :], in1=xt,
                                                    op0=ALU.mult, op1=ALU.add))
                stepped()
                step(nc.vector.bn_stats(stats[:, :], y[:, :]))
                stepped()
                cvt(3)
                nc.vector.bn_aggr(mv[:, :], stats[:, :]).then_inc(var_ready, 1)
                dve.wait_ge(std_ready, t + 1)
                step(nc.vector.reciprocal(rstd[:, :], std[:, :]))
                stepped()
                step(nc.vector.tensor_scalar(xt, y[:, :], mv[:, 0:1], rstd[:, :], ALU.subtract, ALU.mult))
                stepped()
                step(nc.vector.tensor_tensor(prod[:, :, :], x_sb[:, bass.ds(t, 1), :].to_broadcast([P, 3, D]),
                                             avec[:, :, :], ALU.mult))
                stepped()
                nc.vector.tensor_reduce(sd1[:, bass.ds(t, 1), :].rearrange("p o c -> p (o c)"), prod[:, :, :],
                                        AX.X, ALU.add)

            def pair(q, first=False, last=False):
                if first:
                    for c in range(CHUNKS):
                        convert(2, 0, c, True)
                else:
                    finish(2 * q - 1, 1, (lambda c: None) if last else (lambda c: convert(2 * q + 2, 0, c, True)))
                finish(2 * q, 0, (lambda c: None) if last else (lambda c: convert(2 * q + 3, 1, c, True)))

            dve.wait_ge(bias_added, GROUPS)
            pair(0, first=True)
            with dve.Fori(1, PAIRS - 1) as q:
                pair(q)
            pair(PAIRS - 1, last=True)
            finish(TILES - 1, 1, lambda c: None)

        @block.tensor
        def _(pe):
            pe.wait_ge(w_landed, 32)
            pe.wait_ge(ident_ready, 1)
            nc.tensor.transpose(wT_ps[:, 0:P], w0, ident[:, :])
            nc.tensor.transpose(wT_ps[:, P:2 * P], w1, ident[:, :]).then_inc(w_turned, 1)
            pe.wait_ge(w_copied, 1)
            pe.wait_ge(reps_ready, 1)
            nc.tensor.matmul(w0sd_ps, wT[:, 0, :], att_col[:, :], start=True, stop=True)
            for s in range(2):
                nc.tensor.matmul(avec_ps[:, s * D:(s + 1) * D], gat_rep[:, s, :], wT[:, 1, :], start=True, stop=True)
            nc.tensor.matmul(last_ps, last_rep, w1, start=True, stop=True).then_inc(w_made, 1)
            pe.wait_ge(w0sd_ready, 1)

            def turn_x(g):
                if g % 2 == 0:
                    pe.wait_ge(x_landed[g // 2], 16)
                if g >= 2:
                    pe.wait_ge(xT_ready, g - 1)
                for n in range(GROUP):
                    last = nc.tensor.transpose(acc[:, g % 2, n * P:(n + 1) * P], x_sb[:, GROUP * g + n, :], ident[:, :])
                last.then_inc(x_turned, 1)

            turn_x(0)
            for g in range(GROUPS):
                if g + 1 < GROUPS:
                    turn_x(g + 1)
                pe.wait_ge(xT_ready, g + 1)
                if g >= 2:
                    pe.wait_ge(g_ready, g - 1)
                for n in range(GROUP):
                    nc.tensor.matmul(hps[:, g % 2, n * D:(n + 1) * D], xT[g % 2][:, n * P:(n + 1) * P], w0,
                                     start=True, stop=True)
                    last = nc.tensor.matmul(sd_ps[g % 2][:, n, :], xT[g % 2][:, n * P:(n + 1) * P], w0sd[:, :],
                                            start=True, stop=True)
                last.then_inc(h_ready, 1)
            pe.wait_ge(e_in_ready, GROUPS)
            pe.wait_ge(consts_ready, 3)
            pe.wait_ge(ident16_ready, 1)

            def turn_mask(t, s, free, ahead=None):
                if free:
                    pe.wait_ge(stored, t - 1)
                for c in range(CHUNKS):
                    pe.wait_ge(chunk_done, CHUNKS * t + c + 1)
                    rows = mask8[:, s, c * CW:(c + 1) * CW].bitcast(BF16)
                    for n in range(PAIRS // CHUNKS):
                        if ahead and c == CHUNKS - 1 and n == PAIRS // CHUNKS - 1:
                            ahead()
                        last = nc.tensor.transpose(turned[:, s, c * (PAIRS // CHUNKS) + n, :],
                                                   rows[:, n * P:(n + 1) * P], ident16[:, :])
                last.then_inc(mask_turned, 1)

            def ready(t, free):
                pe.wait_ge(staged, t + 1)
                if free:
                    pe.wait_ge(acc_drained, t - 1)

            def aggregate(s):
                for j in range(TILES):
                    last = nc.tensor.matmul(acc[:, s, 0:PARTS * (D + 1)],
                                            stage[:, s, (j // 2) * 2 * P + j % 2:(j // 2 + 1) * 2 * P:2].bitcast(FP8),
                                            parts[:, j, :, :].rearrange("p c f -> p (c f)"),
                                            start=(j == 0), stop=(j == TILES - 1))
                last.then_inc(sums_ready, 1)

            def pair(q, first=False, last=False):
                turn_mask(2 * q + 1, 1, not first, ahead=lambda: ready(2 * q, not first))
                aggregate(0)
                if last:
                    ready(2 * q + 1, True)
                else:
                    turn_mask(2 * q + 2, 0, True, ahead=lambda: ready(2 * q + 1, not first))
                aggregate(1)

            turn_mask(0, 0, False)
            pe.wait_ge(parts_ready, GROUPS)
            pair(0, first=True)
            with pe.Fori(1, PAIRS - 1) as q:
                pair(q)
            pair(PAIRS - 1, last=True)


def layer_two(nc, keep, out_rows):
    store, x1, sd1, lsum, sd0, w_out, ident, flag = (keep[n] for n in (
        "store", "x_sb", "sd1", "lsum", "sd0", "w_out", "ident", "flag"))
    HALF = N // 2
    HT = TILES // 2
    with ExitStack() as ctx:
        sb = lambda name, shape, dt: ctx.enter_context(nc.sbuf_tensor(name, shape, dt))
        sem = lambda name: ctx.enter_context(nc.semaphore(name))
        grow = sb("grow", [P, N], F32)
        ring = sb("ring", [P, 2, 2, HALF], F32)
        held = sb("held", [P, TILES, 3], F32)
        src = sb("src", [P, TILES], F32)
        fac = sb("fac", [P, TILES], F32)
        low = sb("low", [P, TILES], F32)
        nlow = sb("nlow", [P, TILES], F32)
        minus1 = sb("minus1", [P, 1], F32)
        eps = sb("eps2", [P, 1], F32)
        feats = sb("feats", [P, 2, D], F32)
        bad = sb("bad", [P, 3], F32)
        bad1 = sb("bad1", [P, 1], F32)
        ones = sb("ones", [P, 1], F32)
        linv = sb("linv2", [P, GROUPS, GROUP], F32)
        stats = sb("stats2", [P, TILES, 6], F32)
        mv = sb("mv2", [P, TILES, 2], F32)
        rstd = sb("rstd2", [P, TILES], F32)
        shift = sb("shift2", [P, TILES], F32)
        accs = ctx.enter_context(nc.psum_tensor("accs", [P, 8, BANK], F32))
        sumsT = grow
        y = ring[:, :, :, :].rearrange("p a b (t f) -> p (a b t) f", f=D)

        consts_ready, held_ready, exps_ready, nlow_ready, bad_ready, bad_step = (sem(n) for n in (
            "consts_ready2", "held_ready", "exps_ready", "nlow_ready", "bad_ready", "bad_step"))
        bad_summed, flag_ready, spread, grow_ready = (sem(n) for n in ("bad_summed", "flag_ready", "spread", "grow_ready"))
        feats_ready, excess_ready, weights_ready, used, feats_used = (sem(n) for n in (
            "feats_ready", "excess_ready", "weights_ready", "used", "feats_used"))
        acc_done, sums_even, sums_odd, projected, linv_ready, exp_ready, z_ready, y_ready = (sem(n) for n in (
            "acc_done", "sums_even", "sums_odd", "projected", "linv_ready", "exp_ready", "z_ready", "y_ready"))
        chain, var_ready, std_ready, norm_ready, out_act, out_dve, out_done = (sem(n) for n in (
            "chain", "var_ready2", "std_ready2", "norm_ready", "out_act", "out_dve", "out_done"))
        block = ctx.enter_context(nc.Block())

        @block.gpsimd
        def _(pool):
            nc.gpsimd.memset(minus1[:, :], -1.0).then_inc(consts_ready, 1)
            nc.gpsimd.memset(eps[:, :], EPS).then_inc(consts_ready, 1)
            nc.gpsimd.memset(ones[:, :], 1.0).then_inc(consts_ready, 1)
            for g in range(GROUPS):
                pool.wait_ge(z_ready, g + 1)
                yg = y[:, GROUP * g:GROUP * (g + 1), :]
                nc.gpsimd.tensor_tensor(yg, yg, x1[:, GROUP * g:GROUP * (g + 1), :], ALU.add).then_inc(y_ready, 1)

        @block.sync
        def _(sp):
            for g in range(GROUPS):
                if g % 2 == 0:
                    sp.wait_ge(out_act, g // 2 + 1)
                else:
                    sp.wait_ge(out_dve, g // 2 + 1)
                sp.dma_start(out_rows[:, 2 * g:2 * g + 2, :],
                             y[:, GROUP * g:GROUP * (g + 1), :].rearrange("p (q b) f -> p q (b f)", b=2)
                             ).then_inc(out_done, 16)
            sp.wait_ge(out_done, 16 * GROUPS)

        @block.scalar
        def _(act):
            act.wait_ge(held_ready, 1)
            nc.scalar.activation(src[:, :], held[:, :, 0], ACT.Exp, scale=0.99).then_inc(exps_ready, 1)
            nc.scalar.activation(fac[:, :], held[:, :, 1], ACT.Exp, scale=0.99).then_inc(exps_ready, 1)
            nc.scalar.activation(low[:, :], held[:, :, 1], ACT.Exp, scale=0.01).then_inc(exps_ready, 1)
            for c in range(0, 8, 2):
                act.wait_ge(spread, c + 1)
                nc.scalar.copy(grow[:, c * BANK:(c + 1) * BANK], accs[:, c, :]).then_inc(grow_ready, 1)
            act.wait_ge(grow_ready, 8)
            act.wait_ge(consts_ready, 3)
            act.wait_ge(nlow_ready, 1)

            def excess(j, u, first):
                if not first:
                    act.wait_ge(used, 2 * (j - 2) + 2)
                nc.scalar.activation(feats[:, u, 0:D - 1], x1[:, bass.ds(j, 1), 0:D - 1].rearrange("p o f -> p (o f)"),
                                     ACT.Identity, bias=nlow[:, bass.ds(j, 1)], scale=low[:, bass.ds(j, 1)])
                nc.scalar.copy(feats[:, u, D - 1:D], low[:, bass.ds(j, 1)]).then_inc(feats_ready, 1)
                for h in range(2):
                    nc.scalar.activation(ring[:, u, h, :], grow[:, h * HALF:(h + 1) * HALF], ACT.Relu,
                                         bias=minus1[:, :], scale=fac[:, bass.ds(j, 1)]).then_inc(excess_ready, 1)

            for u in range(2):
                excess(u, u, True)
            with act.Fori(1, PAIRS) as q:
                for u in range(2):
                    excess(2 * q + u, u, False)

            for c in range(0, 8, 2):
                act.wait_ge(acc_done, c + 1)
                nc.scalar.copy(sumsT[:, c * BANK:(c + 1) * BANK], accs[:, c, :]).then_inc(sums_even, 1)
            for g in range(GROUPS):
                act.wait_ge(linv_ready, g + 1)
                for n in range(GROUP):
                    last = nc.scalar.activation(y[:, GROUP * g + n, :], accs[:, 2 * (g % 4) + n // 2, 256 * (n % 2):256 * (n % 2) + D],
                                                ACT.Exp, scale=linv[:, g, n:n + 1])
                last.then_inc(exp_ready, 1)
            act.wait_ge(var_ready, 1)
            nc.scalar.activation(rstd[:, :], mv[:, :, 1], ACT.Sqrt, bias=eps[:, :]).then_inc(std_ready, 1)
            act.wait_ge(norm_ready, 1)
            for g in range(0, GROUPS, 2):
                for t in range(GROUP * g, GROUP * (g + 1)):
                    last = nc.scalar.activation(y[:, t, :], y[:, t, :], ACT.Identity, bias=shift[:, t:t + 1],
                                                scale=rstd[:, t:t + 1])
                last.then_inc(out_act, 1)

        @block.vector
        def _(dve):
            nc.vector.tensor_scalar(held[:, :, :], sd1[:, :, :], LIMIT, -LIMIT, ALU.min, ALU.max).then_inc(held_ready, 1)
            nc.vector.tensor_reduce(bad[:, 0:1], sd0[:, :, :].rearrange("p t c -> p (t c)"), AX.X, ALU.max,
                                    apply_absolute_value=True)
            nc.vector.tensor_reduce(bad[:, 1:2], sd1[:, :, 0:2].rearrange("p t c -> p (t c)") if False else sd1[:, :, 0:2],
                                    AX.XY, ALU.max, apply_absolute_value=True)
            nc.vector.tensor_reduce(bad[:, 2:3], lsum[:, :], AX.X, ALU.min).then_inc(bad_step, 1)
            dve.wait_ge(bad_step, 1)
            nc.vector.tensor_scalar(bad[:, 0:2], bad[:, 0:2], LIMIT, None, ALU.is_gt)
            nc.vector.tensor_scalar(bad[:, 2:3], bad[:, 2:3], EMPTY, None, ALU.is_lt).then_inc(bad_step, 1)
            dve.wait_ge(bad_step, 2)
            nc.vector.tensor_reduce(bad1[:, :], bad[:, :], AX.X, ALU.add).then_inc(bad_ready, 1)
            dve.wait_ge(exps_ready, 3)
            nc.vector.scalar_tensor_tensor(out=nlow[:, :], in0=low[:, :], scalar=-1.0, in1=sd1[:, :, 2], op0=ALU.mult,
                                           op1=ALU.mult).then_inc(nlow_ready, 1)
            for c in range(1, 8, 2):
                dve.wait_ge(spread, c + 1)
                nc.vector.tensor_copy(grow[:, c * BANK:(c + 1) * BANK], accs[:, c, :]).then_inc(grow_ready, 1)
            dve.wait_ge(bad_summed, 1)
            nc.vector.tensor_copy(flag[0:1, :], accs[0:1, 7, 0:1]).then_inc(flag_ready, 1)

            def weigh(j, q, u):
                for h in range(2):
                    dve.wait_ge(excess_ready, 2 * j + h + 1)
                    r = ring[:, u, h, :].rearrange("p (t l) -> p t l", l=P)
                    m = store[:, h * HT:(h + 1) * HT, bass.ds(2 * P * q + u, P, 2)]
                    nc.vector.scalar_tensor_tensor(out=r, in0=r, scalar=1.0, in1=m, op0=ALU.add, op1=ALU.mult
                                                   ).then_inc(weights_ready, 1)

            with dve.Fori(0, PAIRS) as q:
                for u in range(2):
                    weigh(2 * q + u, q, u)

            for c in range(1, 8, 2):
                dve.wait_ge(acc_done, c + 1)
                nc.vector.tensor_copy(sumsT[:, c * BANK:(c + 1) * BANK], accs[:, c, :]).then_inc(sums_odd, 1)
            steps = [0]

            def link(ins):
                steps[0] += 1
                ins.then_inc(chain, 1)
                dve.wait_ge(chain, steps[0])

            def statistics(g):
                dve.wait_ge(y_ready, g + 1)
                for t in range(GROUP * g, GROUP * (g + 1)):
                    last = nc.vector.bn_stats(stats[:, t, :], y[:, t, :])
                link(last)
                for t in range(GROUP * g, GROUP * (g + 1)):
                    last = nc.vector.bn_aggr(mv[:, t, :], stats[:, t, :])
                return last

            def invert(g):
                dve.wait_ge(projected, g + 1)
                pr = accs[:, 2 * (g % 4):2 * (g % 4) + 2, :].rearrange("p a (b c) -> p (a b) c", b=2)
                link(nc.vector.tensor_scalar(linv[:, g, :], pr[:, :, D], TINY, None, ALU.max))
                nc.vector.reciprocal(linv[:, g, :], linv[:, g, :]).then_inc(linv_ready, 1)
                return pr

            prs = [invert(0)]
            for g in range(GROUPS):
                if g + 1 < GROUPS:
                    prs.append(invert(g + 1))
                dve.wait_ge(exp_ready, g + 1)
                yg = y[:, GROUP * g:GROUP * (g + 1), :]
                link(nc.vector.tensor_scalar(yg, yg, 1.0, -1.0, ALU.min, ALU.add))
                for n in range(GROUP):
                    last = nc.vector.scalar_tensor_tensor(out=y[:, GROUP * g + n, :], in0=prs[g][:, n, 0:D],
                                                          scalar=linv[:, g, n:n + 1], in1=y[:, GROUP * g + n, :],
                                                          op0=ALU.mult, op1=ALU.max)
                last.then_inc(z_ready, 1)
                if g >= 1:
                    statistics(g - 1)
            statistics(GROUPS - 1).then_inc(var_ready, 1)
            dve.wait_ge(std_ready, 1)
            link(nc.vector.reciprocal(rstd[:, :], rstd[:, :]))
            nc.vector.scalar_tensor_tensor(out=shift[:, :], in0=mv[:, :, 0], scalar=-1.0, in1=rstd[:, :], op0=ALU.mult,
                                           op1=ALU.mult).then_inc(norm_ready, 1)
            dve.wait_ge(norm_ready, 1)
            for g in range(1, GROUPS, 2):
                for t in range(GROUP * g, GROUP * (g + 1)):
                    last = nc.vector.tensor_scalar(y[:, t, :], y[:, t, :], rstd[:, t:t + 1], shift[:, t:t + 1],
                                                   ALU.mult, ALU.add)
                last.then_inc(out_dve, 1)

        @block.tensor
        def _(pe):
            pe.wait_ge(exps_ready, 1)
            for c in range(8):
                for n in range(GROUP):
                    t = c * GROUP + n
                    last = nc.tensor.matmul(accs[:, c, n * P:(n + 1) * P], src[:, t:t + 1].to_broadcast([P, P]),
                                            ident[:, :], start=True, stop=True)
                last.then_inc(spread, 1)
            pe.wait_ge(grow_ready, 8)
            pe.wait_ge(bad_ready, 1)
            pe.wait_ge(consts_ready, 3)
            nc.tensor.matmul(accs[0:1, 7, 0:1], bad1[:, :], ones[:, :], start=True, stop=True).then_inc(bad_summed, 1)
            pe.wait_ge(flag_ready, 1)

            def aggregate(j, u, first=False, last=False):
                for h in range(2):
                    if h == 0:
                        pe.wait_ge(feats_ready, j + 1)
                    pe.wait_ge(weights_ready, 2 * j + h + 1)
                    for c in range(4):
                        ins = nc.tensor.matmul(accs[:, 4 * h + c, :], feats[:, u, :], ring[:, u, h, c * BANK:(c + 1) * BANK],
                                               start=first, stop=last)
                        if last:
                            ins.then_inc(acc_done, 1)
                    if not last:
                        ins.then_inc(used, 1)

            aggregate(0, 0, first=True)
            aggregate(1, 1)
            with pe.Fori(1, PAIRS - 1) as q:
                for u in range(2):
                    aggregate(2 * q + u, u)
            aggregate(TILES - 2, 0)
            aggregate(TILES - 1, 1, last=True)
            for g in range(GROUPS):
                pe.wait_ge(sums_even, g // 2 + 1)
                if g % 2:
                    pe.wait_ge(sums_odd, g // 2 + 1)
                if g < 4:
                    pe.wait_ge(sums_even, g + 1)
                    pe.wait_ge(sums_odd, g + 1)
                else:
                    pe.wait_ge(z_ready, g - 3)
                for n in range(GROUP):
                    t = GROUP * g + n
                    last = nc.tensor.matmul(accs[:, 2 * (g % 4) + n // 2, 256 * (n % 2):256 * (n % 2) + D + 1],
                                            sumsT[:, t * P:(t + 1) * P], w_out[:, :], start=True, stop=True)
                last.then_inc(projected, 1)


def general_layer(nc, ident, flag, x_sb, h_sb, adj, out, w, bias, att_row, b_att, masked, leaky):
    tag = f"general{int(leaky)}_"
    with ExitStack() as ctx:
        sb = lambda name, shape, dt: ctx.enter_context(nc.sbuf_tensor(name, shape, dt))
        sem = lambda name: ctx.enter_context(nc.semaphore(name))
        w_sb, bias_sb, b_att_sb = sb(tag + "w", [P, D], F32), sb(tag + "bias", [P, D], F32), sb(tag + "b_att", [P, 1], F32)
        att_sb = sb(tag + "att", [P, 2, D], F32)
        d_row = sb(tag + "d_row", [P, N], F32)
        logit, mask, adj_t = sb(tag + "logit", [P, N], F32), sb(tag + "mask", [P, N], F32), sb(tag + "adj", [P, N], I32)
        xt, xT, ht = sb(tag + "xt", [P, D], F32), sb(tag + "xT", [P, P], F32), sb(tag + "ht", [P, D], F32)
        prod, sd = sb(tag + "prod", [P, 2, D], F32), sb(tag + "sd", [P, 2], F32)
        s_all = sb(tag + "s", [P, TILES], F32)
        neg_max, total, linv = sb(tag + "neg_max", [P, 1], F32), sb(tag + "total", [P, 1], F32), sb(tag + "linv", [P, 1], F32)
        weightsT = sb(tag + "wT", [P, 2, GROUP * P], F32)
        y, z = sb(tag + "y", [P, D], F32), sb(tag + "z", [P, D], F32)
        mean, var, std = sb(tag + "mean", [P, 1], F32), sb(tag + "var", [P, 1], F32), sb(tag + "std", [P, 1], F32)
        eps = sb(tag + "eps", [P, 1], F32)
        ps = ctx.enter_context(nc.psum_tensor(tag + "ps", [P, 6, BANK], F32))
        x_ps, h_ps, row_ps, sum_ps, turn_ps = ps[:, 0, 0:P], ps[:, 1, 0:D], ps[:, 2, 0:P], ps[:, 3, 0:D], ps[:, 4:6, :]
        (landed, xt_ready, xt_turned, xT_ready, h_done, sd_ready, row_made, row_ready, adj_landed, adj_read,
         max_ready, exp_done, turned, turned_out, summed, low_ready, low_exp, var_ready, std_ready, tile_done, out_done,
         one, two, consts_ready) = (sem(tag + n) for n in (
             "landed", "xt_ready", "xt_turned", "xT_ready", "h_done", "sd_ready", "row_made", "row_ready", "adj_landed",
             "adj_read", "max_ready", "exp_done", "turned", "turned_out", "summed", "low_ready", "low_exp", "var_ready",
             "std_ready", "tile_done", "out_done", "one", "two", "consts_ready"))
        LOADS = 2 + (bias is not None) + (b_att is not None)
        ONE, TWO = 4, 13 + 2 * leaky
        block = ctx.enter_context(nc.Block())

        @block.sync
        def _(sp):
            with sp.If(sp.value_load(flag[0:1, 0:1]) != 0):
                sp.dma_start(w_sb[:, :], w).then_inc(landed, 16)
                sp.dma_start(att_sb[:, :, :].rearrange("p s d -> p (s d)"), att_row.to_broadcast([P, 2 * D])
                             ).then_inc(landed, 16)
                if bias is not None:
                    sp.dma_start(bias_sb[:, :], bias.to_broadcast([P, D])).then_inc(landed, 16)
                if b_att is not None:
                    sp.dma_start(b_att_sb[:, :], b_att.to_broadcast([P, 1])).then_inc(landed, 16)
                sp.dma_start(adj_t[:, :], adj[0]).then_inc(adj_landed, 16)
                with sp.Fori(1, TILES) as t:
                    sp.wait_ge(adj_read, t)
                    sp.dma_start(adj_t[:, :], adj[bass.ds(t, 1)].rearrange("o p j -> p (o j)")).then_inc(adj_landed, 16)
                if out is not None:
                    sp.wait_ge(tile_done, 2 * TILES)
                    sp.dma_start(out.rearrange("(t p) f -> p t f", p=P), x_sb[:, :, :]).then_inc(out_done, 16)
                    sp.wait_ge(out_done, 16)

        @block.gpsimd
        def _(pool):
            with pool.If(pool.value_load(flag[0:1, 0:1]) != 0):
                last = nc.gpsimd.memset(eps[:, :], EPS)
                if bias is None:
                    last = nc.gpsimd.memset(bias_sb[:, :], 0.0)
                if b_att is None:
                    last = nc.gpsimd.memset(b_att_sb[:, :], 0.0)
                last.then_inc(consts_ready, 1)

        @block.scalar
        def _(act):
            with act.If(act.value_load(flag[0:1, 0:1]) != 0):
                act.wait_ge(landed, 16 * LOADS)
                act.wait_ge(consts_ready, 1)
                with act.Fori(0, TILES) as t:
                    act.wait_ge(xt_turned, t + 1)
                    nc.scalar.copy(xT[:, :], x_ps).then_inc(xT_ready, 1)
                    act.wait_ge(row_made, t + 1)
                    nc.scalar.copy(d_row[:, bass.ds(t * P, P)], row_ps).then_inc(row_ready, 1)
                with act.Fori(0, TILES) as t:
                    act.wait_ge(max_ready, t + 1)
                    nc.scalar.activation(logit[:, :], logit[:, :], ACT.Exp, bias=neg_max[:, :]).then_inc(exp_done, 1)
                    for g in range(GROUPS):
                        act.wait_ge(turned, GROUPS * t + g + 1)
                        nc.scalar.copy(weightsT[:, g % 2, :], turn_ps[:, g % 2, :]).then_inc(turned_out, 1)
                    if leaky:
                        act.wait_ge(low_ready, t + 1)
                        nc.scalar.activation(z[:, :], z[:, :], ACT.Exp).then_inc(low_exp, 1)
                    act.wait_ge(var_ready, t + 1)
                    nc.scalar.activation(std[:, :], var[:, :], ACT.Sqrt, bias=eps[:, :], scale=1.0 / D
                                         ).then_inc(std_ready, 1)

        @block.tensor
        def _(pe):
            with pe.If(pe.value_load(flag[0:1, 0:1]) != 0):
                pe.wait_ge(landed, 16 * LOADS)
                with pe.Fori(0, TILES) as t:
                    pe.wait_ge(xt_ready, t + 1)
                    nc.tensor.transpose(x_ps, xt[:, :], ident[:, :]).then_inc(xt_turned, 1)
                    pe.wait_ge(xT_ready, t + 1)
                    nc.tensor.matmul(h_ps, xT[:, :], w_sb[:, :], start=True, stop=True).then_inc(h_done, 1)
                    pe.wait_ge(sd_ready, t + 1)
                    nc.tensor.matmul(row_ps, sd[:, 1:2].to_broadcast([P, P]), ident[:, :], start=True, stop=True
                                     ).then_inc(row_made, 1)
                with pe.Fori(0, TILES) as t:
                    def turn(g):
                        if g == 0:
                            pe.wait_ge(exp_done, t + 1)
                        for n in range(GROUP):
                            j = GROUP * g + n
                            last = nc.tensor.transpose(turn_ps[:, g % 2, n * P:(n + 1) * P], logit[:, j * P:(j + 1) * P],
                                                       ident[:, :])
                        last.then_inc(turned, 1)
                    turn(0)
                    for g in range(GROUPS):
                        if g + 1 < GROUPS:
                            turn(g + 1)
                        pe.wait_ge(turned_out, GROUPS * t + g + 1)
                        for n in range(GROUP):
                            j = GROUP * g + n
                            last = nc.tensor.matmul(sum_ps, weightsT[:, g % 2, n * P:(n + 1) * P], h_sb[:, j, :],
                                                    start=(j == 0), stop=(j == TILES - 1))
                    last.then_inc(summed, 1)

        @block.vector
        def _(dve):
            def links(t, sem_, per_tile):
                n = [0]

                def link(ins):
                    n[0] += 1
                    ins.then_inc(sem_, 1)
                    dve.wait_ge(sem_, per_tile * t + n[0])
                return link

            with dve.If(dve.value_load(flag[0:1, 0:1]) != 0):
                dve.wait_ge(landed, 16 * LOADS)
                dve.wait_ge(consts_ready, 1)
                with dve.Fori(0, TILES) as t:
                    link = links(t, one, ONE)
                    nc.vector.tensor_copy(xt[:, :], x_sb[:, bass.ds(t, 1), :].rearrange("p o f -> p (o f)")
                                          ).then_inc(xt_ready, 1)
                    dve.wait_ge(h_done, t + 1)
                    link(nc.vector.tensor_tensor(ht[:, :], h_ps, bias_sb[:, :], ALU.add))
                    nc.vector.tensor_copy(h_sb[:, bass.ds(t, 1), :].rearrange("p o f -> p (o f)"), ht[:, :])
                    link(nc.vector.tensor_tensor(prod[:, :, :], ht[:, :].rearrange("p (o f) -> p o f", o=1)
                                                 .to_broadcast([P, 2, D]), att_sb[:, :, :], ALU.mult))
                    link(nc.vector.tensor_reduce(sd[:, :], prod[:, :, :], AX.X, ALU.add))
                    link(nc.vector.tensor_scalar(s_all[:, bass.ds(t, 1)], sd[:, 0:1], b_att_sb[:, :], None, ALU.add))
                    nc.vector.tensor_copy(prod[:, 0, 0:1], sd[:, 0:1]).then_inc(sd_ready, 1)
                dve.wait_ge(row_ready, TILES)
                with dve.Fori(0, TILES) as t:
                    link = links(t, two, TWO)
                    dve.wait_ge(adj_landed, 16 * (t + 1))
                    nc.vector.tensor_scalar(mask[:, :], adj_t[:, :], 0.0, None, ALU.is_gt).then_inc(adj_read, 1)
                    link(nc.vector.tensor_scalar(logit[:, :], d_row[:, :], s_all[:, bass.ds(t, 1)], None, ALU.add))
                    if leaky:
                        link(nc.vector.scalar_tensor_tensor(out=logit[:, :], in0=logit[:, :], scalar=0.01,
                                                            in1=logit[:, :], op0=ALU.mult, op1=ALU.max))
                    link(nc.vector.tensor_tensor(logit[:, :], logit[:, :], mask[:, :], ALU.mult))
                    link(nc.vector.tensor_scalar(mask[:, :], mask[:, :], -1.0, masked, ALU.add, ALU.mult))
                    link(nc.vector.tensor_tensor(logit[:, :], logit[:, :], mask[:, :], ALU.add))
                    link(nc.vector.tensor_reduce(total[:, :], logit[:, :], AX.X, ALU.max))
                    nc.vector.tensor_scalar(neg_max[:, :], total[:, :], -1.0, None, ALU.mult).then_inc(max_ready, 1)
                    dve.wait_ge(exp_done, t + 1)
                    link(nc.vector.tensor_reduce(total[:, :], logit[:, :], AX.X, ALU.add))
                    link(nc.vector.reciprocal(linv[:, :], total[:, :]))
                    dve.wait_ge(summed, t + 1)
                    xt_ = x_sb[:, bass.ds(t, 1), :].rearrange("p o f -> p (o f)")
                    if leaky:
                        link(nc.vector.tensor_scalar(y[:, :], sum_ps, linv[:, :], None, ALU.mult))
                        nc.vector.tensor_scalar(z[:, :], y[:, :], 0.0, None, ALU.min).then_inc(low_ready, 1)
                        dve.wait_ge(low_exp, t + 1)
                        link(nc.vector.scalar_tensor_tensor(out=y[:, :], in0=y[:, :], scalar=0.0, in1=z[:, :],
                                                            op0=ALU.max, op1=ALU.add))
                        link(nc.vector.scalar_tensor_tensor(out=y[:, :], in0=y[:, :], scalar=-1.0, in1=xt_,
                                                            op0=ALU.add, op1=ALU.add))
                    else:
                        link(nc.vector.tensor_scalar(z[:, :], sum_ps, linv[:, :], None, ALU.mult))
                        link(nc.vector.tensor_tensor(y[:, :], z[:, :], xt_, ALU.add))
                    link(nc.vector.tensor_reduce(mean[:, :], y[:, :], AX.X, ALU.add))
                    link(nc.vector.tensor_scalar(mean[:, :], mean[:, :], 1.0 / D, None, ALU.mult))
                    link(nc.vector.tensor_scalar(y[:, :], y[:, :], mean[:, :], None, ALU.subtract))
                    link(nc.vector.tensor_tensor(z[:, :], y[:, :], y[:, :], ALU.mult))
                    nc.vector.tensor_reduce(var[:, :], z[:, :], AX.X, ALU.add).then_inc(var_ready, 1)
                    dve.wait_ge(std_ready, t + 1)
                    nc.vector.reciprocal(std[:, :], std[:, :]).then_inc(tile_done, 1)
                    dve.wait_ge(tile_done, 2 * t + 1)
                    nc.vector.tensor_scalar(xt_, y[:, :], std[:, :], None, ALU.mult).then_inc(tile_done, 1)


def general_path(nc, ident, flag, x, adj, w_fc, b_fc, w_att, b_att, w_gat, a_gat, out):
    with ExitStack() as ctx:
        x_sb = ctx.enter_context(nc.sbuf_tensor("g_x", [P, TILES, D], F32))
        h_sb = ctx.enter_context(nc.sbuf_tensor("g_h", [P, TILES, D], F32))
        loaded = ctx.enter_context(nc.semaphore("g_loaded"))
        with nc.Block() as block:
            @block.sync
            def _(sp):
                with sp.If(sp.value_load(flag[0:1, 0:1]) != 0):
                    sp.dma_start(x_sb[:, :, :], x.rearrange("(t p) f -> p t f", p=P)).then_inc(loaded, 16)
                    sp.wait_ge(loaded, 16)
        adj_t = adj.rearrange("(t p) j -> t p j", p=P)
        general_layer(nc, ident, flag, x_sb, h_sb, adj_t, None, w_fc, b_fc.rearrange("(o d) -> o d", o=1),
                      w_att.rearrange("(o d) -> o d", o=1), b_att, 1e9, False)
        general_layer(nc, ident, flag, x_sb, h_sb, adj_t, out, w_gat, None,
                      a_gat.rearrange("d o -> o d"), None, 1e12, True)


def build(nc, x, adj, w_fc, b_fc, w_att, b_att, w_gat, a_gat, out):
    x_rows, adj_rows, out_rows = views(x, adj, out)
    with ExitStack() as last, ExitStack() as ctx:
        keep = {}
        for name, shape, dt in (("ident", [P, P], F32), ("flag", [1, 1], I32)):
            keep[name] = last.enter_context(nc.sbuf_tensor(name, shape, dt))
        for name, shape, dt in (("sd1", [P, TILES, 3], F32),
                                ("lsum", [P, TILES], F32), ("sd0", [P, TILES, 2], F32), ("w_out", [P, D + 1], F32),
                                ("x_sb", [P, TILES, D], F32), ("store", [P, TILES, N], U8)):
            keep[name] = ctx.enter_context(nc.sbuf_tensor(name, shape, dt))
        layer_one(nc, keep, x_rows, adj_rows, w_fc, b_fc, w_att, b_att, w_gat, a_gat)
        layer_two(nc, keep, out_rows)
        ctx.close()
        general_path(nc, keep["ident"], keep["flag"], x, adj, w_fc, b_fc, w_att, b_att, w_gat, a_gat, out)


_INS = ['x', 'adj', 'L0_gnn_W_fc', 'L0_gnn_b_fc', 'L0_gnn_w_att', 'L0_gnn_b_att', 'L1_gnn_W', 'L1_gnn_a']


def kernel(**inputs):
    import numpy as np
    import concourse.bacc as bacc
    from concourse.bass_utils import run_bass_kernel_spmd as run

    nc = bacc.Bacc("TRN2", target_bir_lowering=False, num_devices=1)
    arrays, args = {}, []
    for name in _INS:
        a = np.ascontiguousarray(inputs[name])
        if a.ndim == 0 or name == 'L0_gnn_b_att':
            a = a.reshape(1, 1)
        arrays[f"in_{name}"] = a
        args.append(nc.dram_tensor(f"in_{name}", a.shape, mybir.dt.from_np(a.dtype), kind="ExternalInput").ap())
    out = nc.dram_tensor("out_x", (N, D), F32, kind="ExternalOutput").ap()
    build(nc, *args, out)
    r = run(nc, [arrays], core_ids=[0])
    return r.results[0]["out_x"]
```

```python
from contextlib import ExitStack

import concourse.bass as bass
from concourse import mybir

F32 = mybir.dt.float32
BF16 = mybir.dt.bfloat16
FP8 = mybir.dt.float8e4
U8 = mybir.dt.uint8
U16 = mybir.dt.uint16
I32 = mybir.dt.int32
ALU = mybir.AluOpType
ACT = mybir.ActivationFunctionType
AX = mybir.AxisListType

P = 128
N = 4096
D = 128
TILES = N // P
PAIRS = TILES // 2
CHUNKS = 4
CW = N // CHUNKS
PARTS = 3
GROUP = 4
GROUPS = TILES // GROUP
BANK = 512
MASK_BYTE = 64
LIMIT = 30.0
TINY = 1e-30
EMPTY = 1e-20
EPS = 1e-5


def views(x, adj, out):
    return (x.rearrange("(q k b) f -> k q (b f)", k=P, b=2),
            adj.rearrange("(q k b) j -> q b k j", k=P, b=2),
            out.rearrange("(q k b) f -> k q (b f)", k=P, b=2))


def layer_one(nc, keep, x_rows, adj_rows, w_fc, b_fc, w_att, b_att, w_gat, a_gat):
    store, x_sb, sd1, lsum, sd0, w_out, ident = (keep[n] for n in (
        "store", "x_sb", "sd1", "lsum", "sd0", "w_out", "ident"))
    with ExitStack() as ctx:
        sb = lambda name, shape, dt: ctx.enter_context(nc.sbuf_tensor(name, shape, dt))
        sem = lambda name: ctx.enter_context(nc.semaphore(name))
        parts = sb("parts", [P, TILES, PARTS, D + 1], BF16)
        adj_sb = sb("adj_sb", [P, CHUNKS, CW], I32)
        mask8 = sb("mask8", [P, 2, N], U8)
        stage = sb("stage", [P, 2, N], U8)
        ident16 = sb("ident16", [P, P], BF16)
        w1sd = sb("w1sd", [P, 2], F32)
        bias_row = sb("bias_row", [P, D], F32)
        avec = sb("avec", [P, 3, D], F32)
        dconst = sb("dconst", [P, 2], F32)
        b_att_sb = sb("b_att_sb", [P, 1], F32)
        e_in = sb("e_in", [P, 2, GROUP], F32)
        eps = sb("eps", [P, 1], F32)
        minus_half = sb("minus_half", [P, 1], F32)
        sums = sb("sums", [P, D + 1], F32)
        linv = sb("linv", [P, 1], F32)
        held_l = sb("held_l", [P, 1], F32)
        y = sb("y", [P, D], F32)
        stats = sb("stats", [P, 6], F32)
        mv = sb("mv", [P, 2], F32)
        var = sb("var", [P, 1], F32)
        rstd = sb("rstd", [P, 1], F32)
        prod = sb("prod", [P, 3, D], F32)
        def late(tile, at, shape):
            n = 1
            for m in shape:
                n *= m
            flat = store[:, tile, :].bitcast(F32)[:, at:at + n]
            return flat if len(shape) == 1 else flat.rearrange("p (a c) -> p a c", a=shape[0])

        xT = [late(TILES - 1 - n, 0, [GROUP * P]) for n in range(2)]
        g32 = [late(TILES - 3 - n, 0, [GROUP, D + 1]) for n in range(3)]
        last_rep, att_row, gat_row = late(TILES - 6, 0, [P]), late(TILES - 6, 128, [2, D]), late(TILES - 6, 384, [2, D])
        w0, w1 = late(TILES - 7, 0, [D + 2]), late(TILES - 7, 256, [D])
        w_prod, w_prod1 = late(TILES - 7, 384, [2, D]), late(TILES - 7, 640, [2, D])

        turned = ctx.enter_context(nc.psum_tensor("turned", [P, 2, PAIRS, P], BF16))
        acc = ctx.enter_context(nc.psum_tensor("acc", [P, 2, BANK], F32))
        hps = ctx.enter_context(nc.psum_tensor("hps", [P, 2, BANK], F32))
        h_banks = [hps, turned[:, 1, :, :].rearrange("p q l -> p (q l)").bitcast(F32).rearrange("p (a c) -> p a c", a=2)]
        h_ps = [x[:, :, 0:2 * (D + 2)].rearrange("p a (b c) -> p a b c", b=2) for x in h_banks]
        spare = turned[:, 0, :, :].rearrange("p q l -> p (q l)").bitcast(F32)
        avec_ps, last_ps = spare[:, 0:256], spare[:, 256:384]

        x_landed = [sem(f"x_landed{g}") for g in range(4)]
        w_landed, w1_landed = sem("w_landed"), sem("w1_landed")
        adj_landed = [sem(f"adj_landed{c}") for c in range(CHUNKS)]
        ident_ready, ident16_ready, consts_ready = sem("ident_ready"), sem("ident16_ready"), sem("consts_ready")
        pool_step = sem("pool_step")
        bias_added = sem("bias_added")
        w0_ready, w1sd_ready, w_made = sem("w0_ready"), sem("w1sd_ready"), sem("w_made")
        prep_step = sem("prep_step")
        x_turned, xT_ready, h_ready, e_in_ready, e_ready = (sem(n) for n in (
            "x_turned", "xT_ready", "h_ready", "e_in_ready", "e_ready"))
        g_ready, hi_ready, rest_ready, mid_ready, parts_ready = (sem(n) for n in (
            "g_ready", "hi_ready", "rest_ready", "mid_ready", "parts_ready"))
        chunk_done, mask_turned, staged, stored, sums_ready = (sem(n) for n in (
            "chunk_done", "mask_turned", "staged", "stored", "sums_ready"))
        acc_drained, tile_step, var_ready, var_step, rstd_ready, w_read = (sem(n) for n in (
            "acc_drained", "tile_step", "var_ready", "var_step", "rstd_ready", "w_read"))
        STEPS = 6

        block = ctx.enter_context(nc.Block())

        @block.sync
        def _(sp):
            for g in range(4):
                if g == 1:
                    sp.wait_ge(w_landed, 16 * 4)
                sp.dma_start(x_sb[:, 8 * g:8 * g + 8, :].rearrange("p (q b) f -> p q (b f)", b=2),
                             x_rows[:, 4 * g:4 * g + 4, :]).then_inc(x_landed[g], 16)

            def load(q, first=False):
                for b in range(2):
                    for c in range(CHUNKS):
                        if not (first and b == 0):
                            sp.wait_ge(chunk_done, q * 2 * CHUNKS + (b - 1) * CHUNKS + c + 1)
                        sp.dma_start(adj_sb[:, c, :],
                                     adj_rows[q, b, :, c * CW:(c + 1) * CW]).then_inc(adj_landed[c], 16)

            load(0, first=True)
            with sp.Fori(1, PAIRS) as q:
                load(q)

        @block.gpsimd
        def _(pool):
            nc.gpsimd.memset(ident[:, :], 0.0).then_inc(pool_step, 1)
            pool.wait_ge(pool_step, 1)
            nc.gpsimd.affine_select(out=ident[:, :], in_=ident[:, :], compare_op=ALU.not_equal, fill=1.0,
                                    base=0, pattern=[[-1, P]], channel_multiplier=1).then_inc(ident_ready, 1)
            pool.wait_ge(ident_ready, 1)
            nc.gpsimd.tensor_copy(ident16[:, :], ident[:, :]).then_inc(ident16_ready, 1)
            nc.gpsimd.memset(eps[:, :], EPS).then_inc(consts_ready, 1)
            nc.gpsimd.memset(avec[:, 2, :], 1.0 / D).then_inc(consts_ready, 1)
            nc.gpsimd.memset(minus_half[:, :], -0.5).then_inc(consts_ready, 1)
            for g in range(GROUPS):
                pool.wait_ge(hi_ready, g + 1)
                nc.gpsimd.tensor_tensor(g32[g % 3], g32[g % 3], parts[:, GROUP * g:GROUP * (g + 1), 0, :],
                                        ALU.subtract).then_inc(rest_ready, 1)
            pool.wait_ge(w_landed, 16 * 4)
            pool.wait_ge(x_turned, GROUPS)
            for g in range(GROUPS):
                xg = x_sb[:, GROUP * g:GROUP * (g + 1), :]
                nc.gpsimd.tensor_tensor(xg, xg, bias_row[:, :].rearrange("p (o d) -> p o d", o=1).to_broadcast(
                    [P, GROUP, D]), ALU.add).then_inc(bias_added, 1)

            def root(t):
                pool.wait_ge(var_ready, t + 1)
                nc.gpsimd.tensor_tensor(var[:, :], mv[:, 1:2], eps[:, :], ALU.add).then_inc(var_step, 1)
                pool.wait_ge(var_step, t + 1)
                nc.gpsimd.tensor_tensor(rstd[:, :], var[:, :], minus_half[:, :], ALU.pow).then_inc(rstd_ready, 1)

            with pool.Fori(0, TILES) as t:
                root(t)

        @block.scalar
        def _(act):
            act.dma_start(w0[:, 0:D], w_fc).then_inc(w_landed, 16)
            act.dma_start(att_row.rearrange("p s d -> p (s d)"),
                          w_att.rearrange("(o d) -> o d", o=1).to_broadcast([P, 2 * D])).then_inc(w_landed, 16)
            act.dma_start(bias_row[:, :], b_fc.rearrange("(o d) -> o d", o=1).to_broadcast([P, D])
                          ).then_inc(w_landed, 16)
            act.dma_start(b_att_sb[:, :], b_att.to_broadcast([P, 1])).then_inc(w_landed, 16)
            act.dma_start(w1, w_gat).then_inc(w1_landed, 16)
            act.dma_start(gat_row.rearrange("p s d -> p (s d)"), a_gat.rearrange("d o -> o d").to_broadcast([P, 2 * D])
                          ).then_inc(w1_landed, 16)

            def turn_out(g):
                act.wait_ge(x_turned, g + 1)
                if g >= 2:
                    act.wait_ge(h_ready, g - 1)
                nc.scalar.copy(xT[g % 2], acc[:, g % 2, :]).then_inc(xT_ready, 1)

            def exp_logits(g):
                act.wait_ge(e_in_ready, g + 1)
                if g >= 3:
                    act.wait_ge(parts_ready, g - 2)
                nc.scalar.activation(g32[g % 3][:, :, D], e_in[:, g % 2, :], ACT.Exp).then_inc(e_ready, 1)

            def first_part(g):
                act.wait_ge(g_ready, g + 1)
                nc.scalar.copy(parts[:, GROUP * g:GROUP * (g + 1), 0, :], g32[g % 3]).then_inc(hi_ready, 1)

            def middle_part(g):
                act.wait_ge(rest_ready, g + 1)
                nc.scalar.copy(parts[:, GROUP * g:GROUP * (g + 1), 1, :], g32[g % 3]).then_inc(mid_ready, 1)

            def stage_mask(t, s, free):
                act.wait_ge(mask_turned, t + 1)
                if free:
                    act.wait_ge(sums_ready, t - 1)
                nc.scalar.copy(stage[:, s, :].bitcast(U16),
                               turned[:, s].rearrange("p q l -> p (q l)").bitcast(U16)).then_inc(staged, 1)

            def store_mask(t, s):
                nc.scalar.copy(store[:, bass.ds(t, 1), :].rearrange("p t n -> p (t n)").bitcast(U16),
                               turned[:, s].rearrange("p q l -> p (q l)").bitcast(U16)).then_inc(stored, 1)

            def pair(q, first=False, last=False):
                stage_mask(2 * q + 1, 1, not first)
                store_mask(2 * q + 1, 1)
                if not last:
                    stage_mask(2 * q + 2, 0, True)
                    store_mask(2 * q + 2, 0)

            turn_out(0)
            turn_out(1)
            exp_logits(0)
            for g in range(GROUPS):
                if g + 2 < GROUPS:
                    turn_out(g + 2)
                first_part(g)
                if g + 1 < GROUPS:
                    exp_logits(g + 1)
                if g >= 1:
                    middle_part(g - 1)
                if g == GROUPS - 2:
                    stage_mask(0, 0, False)
            middle_part(GROUPS - 1)
            store_mask(0, 0)
            pair(0, first=True)
            with act.Fori(1, PAIRS - 1) as q:
                pair(q)
            pair(PAIRS - 1, last=True)

        @block.vector
        def _(dve):
            steps = [0]

            def link(ins):
                steps[0] += 1
                ins.then_inc(prep_step, 1)
                dve.wait_ge(prep_step, steps[0])

            dve.wait_ge(w_landed, 16 * 4)
            link(nc.vector.tensor_tensor(w_prod, att_row, w0[:, 0:D].rearrange("p (o d) -> p o d", o=1)
                                         .to_broadcast([P, 2, D]), ALU.mult))
            nc.vector.tensor_reduce(w0[:, D:D + 2], w_prod, AX.X, ALU.add).then_inc(w0_ready, 1)
            link(nc.vector.tensor_tensor(att_row, att_row, bias_row[:, :].rearrange("p (o d) -> p o d", o=1)
                                         .to_broadcast([P, 2, D]), ALU.mult))
            link(nc.vector.tensor_reduce(dconst[:, :], att_row, AX.X, ALU.add))
            link(nc.vector.tensor_tensor(dconst[:, 0:1], dconst[:, 0:1], b_att_sb[:, :], ALU.add))

            def convert(t, s, c, free):
                dve.wait_ge(adj_landed[c], 16 * (t + 1))
                if free and c == 0:
                    dve.wait_ge(mask_turned, t - 1)
                nc.vector.tensor_scalar(mask8[:, s, c * CW:(c + 1) * CW], adj_sb[:, c, :], 0.0, float(MASK_BYTE),
                                        ALU.is_gt, ALU.mult).then_inc(chunk_done, 1)

            def logits(g):
                dve.wait_ge(h_ready, g + 1)
                gs = slice(GROUP * g, GROUP * (g + 1))
                link(nc.vector.tensor_tensor(sd0[:, gs, :].rearrange("p (a b) c -> p a b c", b=2), h_ps[g % 2][:, :, :, D:D + 2],
                                             dconst[:, :].rearrange("p (a b c) -> p a b c", a=1, b=1)
                                             .to_broadcast([P, 2, 2, 2]), ALU.add))
                if g >= 2:
                    dve.wait_ge(e_ready, g - 1)
                nc.vector.tensor_scalar(e_in[:, g % 2, :], sd0[:, gs, 1], LIMIT, -LIMIT, ALU.min, ALU.max
                                        ).then_inc(e_in_ready, 1)

            def last_part(g):
                dve.wait_ge(mid_ready, g + 1)
                gs = slice(GROUP * g, GROUP * (g + 1))
                nc.vector.tensor_tensor(parts[:, gs, 2, :], g32[g % 3], parts[:, gs, 1, :], ALU.subtract
                                        ).then_inc(parts_ready, 1)

            def second_weights():
                dve.wait_ge(w1_landed, 32)
                nc.vector.tensor_copy(last_rep, ident[:, P - 1:P].to_broadcast([P, P]))
                link(nc.vector.tensor_tensor(w_prod1, gat_row, w1.rearrange("p (o d) -> p o d", o=1)
                                             .to_broadcast([P, 2, D]), ALU.mult))
                nc.vector.tensor_reduce(w1sd[:, :], w_prod1, AX.X, ALU.add).then_inc(w1sd_ready, 1)

            def take_second_weights():
                dve.wait_ge(w_made, 1)
                nc.vector.tensor_copy(avec[:, 0:2, :], avec_ps.rearrange("p (s d) -> p s d", s=2))
                nc.vector.tensor_tensor(w_out[:, 0:D], w1, last_ps, ALU.subtract).then_inc(w_read, 1)
                nc.vector.tensor_copy(w_out[:, D:D + 1], ident[:, P - 1:P]).then_inc(consts_ready, 1)

            logits(0)
            for g in range(GROUPS):
                dve.wait_ge(e_ready, g + 1)
                gg = g32[g % 3]
                gv = gg.rearrange("p (a b) c -> p a b c", b=2)
                nc.vector.tensor_tensor(gv[:, :, :, 0:D], h_ps[g % 2][:, :, :, 0:D],
                                        gv[:, :, :, D:D + 1].to_broadcast([P, 2, 2, D]), ALU.mult).then_inc(g_ready, 1)
                if g + 1 < GROUPS:
                    logits(g + 1)
                if g == 1:
                    second_weights()
                if g == 3:
                    take_second_weights()
                if g >= 2:
                    last_part(g - 2)
                if g >= GROUPS - CHUNKS:
                    convert(0, 0, g - (GROUPS - CHUNKS), False)
            last_part(GROUPS - 2)
            last_part(GROUPS - 1)
            for c in range(CHUNKS):
                convert(1, 1, c, False)

            def finish(t, s, cvt):
                def step(ins):
                    n[0] += 1
                    ins.then_inc(tile_step, 1)

                def stepped():
                    dve.wait_ge(tile_step, STEPS * t + n[0])
                n = [0]
                dve.wait_ge(sums_ready, t + 1)
                nc.vector.tensor_reduce(sums[:, :], acc[:, s, 0:PARTS * (D + 1)].rearrange(
                    "p (c f) -> p f c", c=PARTS), AX.X, ALU.add).then_inc(acc_drained, 1)
                cvt(0)
                dve.wait_ge(acc_drained, t + 1)
                step(nc.vector.tensor_scalar(held_l[:, :], sums[:, D:D + 1], TINY, None, ALU.max))
                cvt(1)
                stepped()
                step(nc.vector.reciprocal(linv[:, :], held_l[:, :]))
                nc.vector.tensor_copy(lsum[:, bass.ds(t, 1)], held_l[:, :])
                cvt(2)
                stepped()
                xt = x_sb[:, bass.ds(t, 1), :].rearrange("p o f -> p (o f)")
                step(nc.vector.scalar_tensor_tensor(out=y[:, :], in0=sums[:, 0:D], scalar=linv[:, :], in1=xt,
                                                    op0=ALU.mult, op1=ALU.add))
                stepped()
                step(nc.vector.bn_stats(stats[:, :], y[:, :]))
                stepped()
                cvt(3)
                nc.vector.bn_aggr(mv[:, :], stats[:, :]).then_inc(var_ready, 1)
                dve.wait_ge(rstd_ready, t + 1)
                step(nc.vector.tensor_scalar(xt, y[:, :], mv[:, 0:1], rstd[:, :], ALU.subtract, ALU.mult))
                stepped()
                step(nc.vector.tensor_tensor(prod[:, :, :], x_sb[:, bass.ds(t, 1), :].to_broadcast([P, 3, D]),
                                             avec[:, :, :], ALU.mult))
                stepped()
                nc.vector.tensor_reduce(sd1[:, bass.ds(t, 1), :].rearrange("p o c -> p (o c)"), prod[:, :, :],
                                        AX.X, ALU.add)

            def pair(q, first=False, last=False):
                if first:
                    for c in range(CHUNKS):
                        convert(2, 0, c, True)
                    dve.wait_ge(bias_added, GROUPS)
                else:
                    finish(2 * q - 1, 1, (lambda c: None) if last else (lambda c: convert(2 * q + 2, 0, c, True)))
                finish(2 * q, 0, (lambda c: None) if last else (lambda c: convert(2 * q + 3, 1, c, True)))

            pair(0, first=True)
            with dve.Fori(1, PAIRS - 1) as q:
                pair(q)
            pair(PAIRS - 1, last=True)
            finish(TILES - 1, 1, lambda c: None)

        @block.tensor
        def _(pe):
            def turn_x(g):
                if g % 2 == 0:
                    pe.wait_ge(x_landed[g // 2], 16)
                if g >= 2:
                    pe.wait_ge(xT_ready, g - 1)
                for n in range(GROUP):
                    last = nc.tensor.transpose(acc[:, g % 2, n * P:(n + 1) * P], x_sb[:, GROUP * g + n, :], ident[:, :])
                last.then_inc(x_turned, 1)

            def turn_mask(t, s, free, ahead=None):
                if free:
                    pe.wait_ge(stored, t - 1)
                for c in range(CHUNKS):
                    pe.wait_ge(chunk_done, CHUNKS * t + c + 1)
                    rows = mask8[:, s, c * CW:(c + 1) * CW].bitcast(BF16)
                    for n in range(PAIRS // CHUNKS):
                        if ahead and c == CHUNKS - 1 and n == PAIRS // CHUNKS - 1:
                            ahead()
                        last = nc.tensor.transpose(turned[:, s, c * (PAIRS // CHUNKS) + n, :],
                                                   rows[:, n * P:(n + 1) * P], ident16[:, :])
                last.then_inc(mask_turned, 1)

            def ready(t, free):
                pe.wait_ge(staged, t + 1)
                if free:
                    pe.wait_ge(acc_drained, t - 1)

            def aggregate(s):
                for j in range(TILES):
                    last = nc.tensor.matmul(acc[:, s, 0:PARTS * (D + 1)],
                                            stage[:, s, (j // 2) * 2 * P + j % 2:(j // 2 + 1) * 2 * P:2].bitcast(FP8),
                                            parts[:, j, :, :].rearrange("p c f -> p (c f)"),
                                            start=(j == 0), stop=(j == TILES - 1))
                last.then_inc(sums_ready, 1)

            def pair(q, first=False, last=False):
                if first:
                    ready(0, False)
                else:
                    turn_mask(2 * q + 1, 1, True, ahead=lambda: ready(2 * q, True))
                aggregate(0)
                if last:
                    ready(2 * q + 1, True)
                else:
                    turn_mask(2 * q + 2, 0, True, ahead=lambda: ready(2 * q + 1, not first))
                aggregate(1)

            pe.wait_ge(ident_ready, 1)
            turn_x(0)
            turn_x(1)
            pe.wait_ge(w0_ready, 1)
            for g in range(GROUPS):
                pe.wait_ge(xT_ready, g + 1)
                if g >= 2:
                    pe.wait_ge(g_ready, g - 1)
                for n in range(GROUP):
                    last = nc.tensor.matmul(h_ps[g % 2][:, n // 2, n % 2, :], xT[g % 2][:, n * P:(n + 1) * P], w0,
                                            start=True, stop=True)
                last.then_inc(h_ready, 1)
                if g + 2 < GROUPS:
                    turn_x(g + 2)
                if g == 2:
                    pe.wait_ge(w1sd_ready, 1)
                    for c in range(2):
                        nc.tensor.matmul(avec_ps[:, c * D:(c + 1) * D], w1sd[:, c:c + 1].to_broadcast([P, P]),
                                         ident[:, :], start=True, stop=True)
                    nc.tensor.matmul(last_ps, last_rep, w1, start=True, stop=True).then_inc(w_made, 1)
            pe.wait_ge(ident16_ready, 1)
            pe.wait_ge(w_read, 1)
            turn_mask(0, 0, False)
            pe.wait_ge(g_ready, GROUPS)
            turn_mask(1, 1, False)
            pe.wait_ge(parts_ready, GROUPS)
            pair(0, first=True)
            with pe.Fori(1, PAIRS - 1) as q:
                pair(q)
            pair(PAIRS - 1, last=True)


def layer_two(nc, keep, out_rows):
    store, x1, sd1, lsum, sd0, w_out, ident, flag = (keep[n] for n in (
        "store", "x_sb", "sd1", "lsum", "sd0", "w_out", "ident", "flag"))
    BANKS = (5, 3)
    FIRST = (0, BANKS[0])
    NB, NB2 = BANKS
    CHUNKS = ((0, 3), (3, NB))
    NC = len(CHUNKS)
    DEEP = 3
    with ExitStack() as ctx:
        sb = lambda name, shape, dt: ctx.enter_context(nc.sbuf_tensor(name, shape, dt))
        sem = lambda name: ctx.enter_context(nc.semaphore(name))
        grow = sb("grow", [P, N], F32)
        ring = sb("ring", [P, 2 * NB * BANK], F32)
        y = sb("y2", [P, TILES, D], F32)
        held = sb("held", [P, TILES, 3], F32)
        src = sb("src", [P, TILES], F32)
        fac = sb("fac", [P, TILES], F32)
        low = sb("low", [P, TILES], F32)
        nlow = sb("nlow", [P, TILES], F32)
        minus1 = sb("minus1", [P, 1], F32)
        eps = sb("eps2", [P, TILES], F32)
        minus_half = sb("minus_half2", [P, TILES], F32)
        feats = sb("feats", [P, 2 + DEEP, D], F32)
        bad = sb("bad", [P, 3], F32)
        bad1 = sb("bad1", [P, 1], F32)
        ones = sb("ones", [P, 1], F32)
        linv = sb("linv2", [P, GROUPS, GROUP], F32)
        stats = sb("stats2", [P, TILES, 6], F32)
        mv = sb("mv2", [P, TILES, 2], F32)
        var = sb("var2", [P, TILES], F32)
        rstd = sb("rstd2", [P, TILES], F32)
        shift = sb("shift2", [P, TILES], F32)
        accs = ctx.enter_context(nc.psum_tensor("accs", [P, 8, BANK], F32))
        sumsT = grow

        consts_ready, held_ready, exps_ready, nlow_ready, bad_ready, bad_step = (sem(n) for n in (
            "consts_ready2", "held_ready", "exps_ready", "nlow_ready", "bad_ready", "bad_step"))
        bad_summed, flag_ready, spread = (sem(n) for n in ("bad_summed", "flag_ready", "spread"))
        grow_act, grow_dve, sums_act, sums_dve = (sem(n) for n in ("grow_act", "grow_dve", "sums_act", "sums_dve"))
        feats_ready, excess_ready, weights_ready, used = (sem(n) for n in (
            "feats_ready", "excess_ready", "weights_ready", "used"))
        acc_done, projected, linv_ready, exp_ready, z_ready, y_ready = (sem(n) for n in (
            "acc_done", "projected", "linv_ready", "exp_ready", "z_ready", "y_ready"))
        chain, var_ready, var_step, rstd_ready, shift_ready, out_act, out_dve, out_done = (sem(n) for n in (
            "chain", "var_ready2", "var_step2", "rstd_ready2", "shift_ready", "out_act", "out_dve", "out_done"))
        block = ctx.enter_context(nc.Block())

        def shared(share, c):
            return c % 2 == 0, (FIRST[share] and (NB + 1) // 2) + c // 2 + 1 if c % 2 == 0 else \
                (FIRST[share] and NB // 2) + c // 2 + 1

        def copied(eng, share, c, by_act, by_dve):
            mine, count = shared(share, c)
            eng.wait_ge(by_act if mine else by_dve, count)

        def slots(g):
            return accs[:, 2 * (g % 2):2 * (g % 2) + 2, :].rearrange("p a (b c) -> p (a b) c", b=2)

        def rows(g):
            return slice(GROUP * g, GROUP * (g + 1))

        @block.gpsimd
        def _(pool):
            nc.gpsimd.memset(minus1[:, :], -1.0).then_inc(consts_ready, 1)
            nc.gpsimd.memset(eps[:, :], EPS).then_inc(consts_ready, 1)
            nc.gpsimd.memset(minus_half[:, :], -0.5).then_inc(consts_ready, 1)
            nc.gpsimd.memset(ones[:, :], 1.0).then_inc(consts_ready, 1)
            pool.wait_ge(consts_ready, 4)

            def root(g):
                pool.wait_ge(var_ready, g + 1)
                nc.gpsimd.tensor_tensor(var[:, rows(g)], mv[:, rows(g), 1], eps[:, rows(g)], ALU.add).then_inc(var_step, 1)
                pool.wait_ge(var_step, g + 1)
                nc.gpsimd.tensor_tensor(rstd[:, rows(g)], var[:, rows(g)], minus_half[:, rows(g)], ALU.pow
                                        ).then_inc(rstd_ready, 1)

            for g in range(GROUPS):
                pool.wait_ge(z_ready, g + 1)
                nc.gpsimd.tensor_tensor(y[:, rows(g), :], y[:, rows(g), :], x1[:, rows(g), :], ALU.add).then_inc(y_ready, 1)
                if g < NB:
                    root(g)
                elif g > NB:
                    root(g - 1)
            root(GROUPS - 1)

        @block.sync
        def _(sp):
            for g in range(GROUPS):
                sp.wait_ge(out_dve, g + 1)
                if g >= NB:
                    sp.wait_ge(out_act, g - NB + 1)
                sp.dma_start(out_rows[:, 2 * g:2 * g + 2, :],
                             y[:, rows(g), :].rearrange("p (q b) f -> p q (b f)", b=2)).then_inc(out_done, 16)
            sp.wait_ge(out_done, 16 * GROUPS)

        @block.scalar
        def _(act):
            act.wait_ge(held_ready, 1)
            nc.scalar.activation(src[:, :], held[:, :, 0], ACT.Exp, scale=0.99).then_inc(exps_ready, 1)
            nc.scalar.activation(fac[:, :], held[:, :, 1], ACT.Exp, scale=0.99).then_inc(exps_ready, 1)
            nc.scalar.activation(low[:, :], held[:, :, 1], ACT.Exp, scale=0.01).then_inc(exps_ready, 1)

            def grow_out(share):
                for c in range(0, BANKS[share], 2):
                    b = FIRST[share] + c
                    act.wait_ge(spread, b + 1)
                    nc.scalar.copy(grow[:, b * BANK:(b + 1) * BANK], accs[:, b, :]).then_inc(grow_act, 1)

            def sums_out(share):
                for c in range(0, BANKS[share], 2):
                    b = FIRST[share] + c
                    act.wait_ge(acc_done, b + 1)
                    nc.scalar.copy(sumsT[:, b * BANK:(b + 1) * BANK], accs[:, b, :]).then_inc(sums_act, 1)

            def features(j, u):
                nc.scalar.activation(feats[:, u, 0:D - 1], x1[:, bass.ds(j, 1), 0:D - 1].rearrange("p o f -> p (o f)"),
                                     ACT.Identity, bias=nlow[:, bass.ds(j, 1)], scale=low[:, bass.ds(j, 1)])
                nc.scalar.copy(feats[:, u, D - 1:D], low[:, bass.ds(j, 1)]).then_inc(feats_ready, 1)

            def excess(j, at, banks):
                nc.scalar.activation(ring[:, at:at + (banks[1] - banks[0]) * BANK],
                                     grow[:, banks[0] * BANK:banks[1] * BANK], ACT.Relu,
                                     bias=minus1[:, :], scale=fac[:, bass.ds(j, 1)]).then_inc(excess_ready, 1)

            def first_share(j, u, free=True):
                if free:
                    act.wait_ge(used, NC * (j - 2) + 1)
                excess(j, u * NB * BANK, CHUNKS[0])
                if free:
                    act.wait_ge(used, NC * (j - 1))
                features(j, u)
                excess(j, (u * NB + CHUNKS[1][0]) * BANK, CHUNKS[1])

            def second_share(j):
                u = j % DEEP
                if j == 0:
                    act.wait_ge(used, NC * (TILES - 1))
                elif j < DEEP:
                    act.wait_ge(acc_done, min(NB, (j + 1) * NB2 - NB))
                else:
                    act.wait_ge(used, NC * (TILES - 1) + j - DEEP + 1)
                features(j, 2 + u)
                excess(j, u * NB2 * BANK, (NB, NB + NB2))

            def exp_out(g):
                act.wait_ge(linv_ready, g + 1)
                for n in range(GROUP):
                    last = nc.scalar.activation(y[:, GROUP * g + n, :], slots(g)[:, n, 0:D], ACT.Exp,
                                                scale=linv[:, g, n:n + 1])
                last.then_inc(exp_ready, 1)

            grow_out(0)
            act.wait_ge(grow_act, (NB + 1) // 2)
            act.wait_ge(grow_dve, NB // 2)
            act.wait_ge(consts_ready, 4)
            act.wait_ge(nlow_ready, 1)
            first_share(0, 0, free=False)
            first_share(1, 1, free=False)
            grow_out(1)
            with act.Fori(1, PAIRS) as q:
                first_share(2 * q, 0)
                first_share(2 * q + 1, 1)
            act.wait_ge(grow_act, (NB + 1) // 2 + (NB2 + 1) // 2)
            act.wait_ge(grow_dve, NB // 2 + NB2 // 2)
            for q in range(PAIRS):
                second_share(2 * q)
                if q == 0:
                    sums_out(0)
                second_share(2 * q + 1)
                if q % 2 == 1 and q // 2 < NB:
                    exp_out(q // 2)
            sums_out(1)
            for g in range(NB, GROUPS):
                exp_out(g)
            for g in range(NB, GROUPS):
                act.wait_ge(shift_ready, g + 1)
                for t in range(GROUP * g, GROUP * g + GROUP // 2):
                    last = nc.scalar.activation(y[:, t, :], y[:, t, :], ACT.Identity, bias=shift[:, t:t + 1],
                                                scale=rstd[:, t:t + 1])
                last.then_inc(out_act, 1)

        @block.vector
        def _(dve):
            nc.vector.tensor_scalar(held[:, :, :], sd1[:, :, :], LIMIT, -LIMIT, ALU.min, ALU.max).then_inc(held_ready, 1)
            nc.vector.tensor_reduce(bad[:, 0:1], sd0[:, :, :], AX.XY, ALU.max, apply_absolute_value=True)
            nc.vector.tensor_reduce(bad[:, 1:2], sd1[:, :, 0:2], AX.XY, ALU.max, apply_absolute_value=True)
            nc.vector.tensor_reduce(bad[:, 2:3], lsum[:, :], AX.X, ALU.min).then_inc(bad_step, 1)
            dve.wait_ge(bad_step, 1)
            nc.vector.tensor_scalar(bad[:, 0:2], bad[:, 0:2], LIMIT, None, ALU.is_gt)
            nc.vector.tensor_scalar(bad[:, 2:3], bad[:, 2:3], EMPTY, None, ALU.is_lt).then_inc(bad_step, 1)
            dve.wait_ge(bad_step, 2)
            nc.vector.tensor_reduce(bad1[:, :], bad[:, :], AX.X, ALU.add).then_inc(bad_ready, 1)
            dve.wait_ge(exps_ready, 3)
            nc.vector.scalar_tensor_tensor(out=nlow[:, :], in0=low[:, :], scalar=-1.0, in1=sd1[:, :, 2], op0=ALU.mult,
                                           op1=ALU.mult).then_inc(nlow_ready, 1)

            def grow_out(share):
                for c in range(1, BANKS[share], 2):
                    b = FIRST[share] + c
                    dve.wait_ge(spread, b + 1)
                    nc.vector.tensor_copy(grow[:, b * BANK:(b + 1) * BANK], accs[:, b, :]).then_inc(grow_dve, 1)

            def sums_out(share):
                for c in range(1, BANKS[share], 2):
                    b = FIRST[share] + c
                    dve.wait_ge(acc_done, b + 1)
                    nc.vector.tensor_copy(sumsT[:, b * BANK:(b + 1) * BANK], accs[:, b, :]).then_inc(sums_dve, 1)

            def weigh(q, u, at, banks, count):
                dve.wait_ge(excess_ready, count)
                r = ring[:, at:at + (banks[1] - banks[0]) * BANK].rearrange("p (t l) -> p t l", l=P)
                m = store[:, banks[0] * GROUP:banks[1] * GROUP, bass.ds(2 * P * q + u, P, 2)]
                nc.vector.scalar_tensor_tensor(out=r, in0=r, scalar=1.0, in1=m, op0=ALU.add, op1=ALU.mult
                                               ).then_inc(weights_ready, 1)

            def first_share(q):
                for u in range(2):
                    for c, banks in enumerate(CHUNKS):
                        weigh(q, u, (u * NB + banks[0]) * BANK, banks, NC * (2 * q + u) + c + 1)

            def second_share(q, u):
                j = 2 * q + u
                weigh(q, u, j % DEEP * NB2 * BANK, (NB, NB + NB2), NC * TILES + j + 1)

            steps = [0]

            def link(ins):
                steps[0] += 1
                ins.then_inc(chain, 1)
                dve.wait_ge(chain, steps[0])

            def invert(g):
                dve.wait_ge(projected, g + 1)
                link(nc.vector.tensor_scalar(linv[:, g, :], slots(g)[:, :, D], TINY, None, ALU.max))
                nc.vector.reciprocal(linv[:, g, :], linv[:, g, :]).then_inc(linv_ready, 1)

            def elu(g):
                dve.wait_ge(exp_ready, g + 1)
                link(nc.vector.tensor_scalar(y[:, rows(g), :], y[:, rows(g), :], 1.0, -1.0, ALU.min, ALU.add))
                for n in range(GROUP):
                    last = nc.vector.scalar_tensor_tensor(out=y[:, GROUP * g + n, :], in0=slots(g)[:, n, 0:D],
                                                          scalar=linv[:, g, n:n + 1], in1=y[:, GROUP * g + n, :],
                                                          op0=ALU.mult, op1=ALU.max)
                last.then_inc(z_ready, 1)

            def statistics(g):
                dve.wait_ge(y_ready, g + 1)
                for t in range(GROUP * g, GROUP * (g + 1)):
                    last = nc.vector.bn_stats(stats[:, t, :], y[:, t, :])
                link(last)
                for t in range(GROUP * g, GROUP * (g + 1)):
                    last = nc.vector.bn_aggr(mv[:, t, :], stats[:, t, :])
                last.then_inc(var_ready, 1)

            def norm(g):
                dve.wait_ge(rstd_ready, g + 1)
                nc.vector.scalar_tensor_tensor(out=shift[:, rows(g)], in0=mv[:, rows(g), 0], scalar=-1.0,
                                               in1=rstd[:, rows(g)], op0=ALU.mult, op1=ALU.mult).then_inc(shift_ready, 1)
                dve.wait_ge(shift_ready, g + 1)
                for t in range(GROUP * g + (0 if g < NB else GROUP // 2), GROUP * (g + 1)):
                    last = nc.vector.tensor_scalar(y[:, t, :], y[:, t, :], rstd[:, t:t + 1], shift[:, t:t + 1],
                                                   ALU.mult, ALU.add)
                last.then_inc(out_dve, 1)

            grow_out(0)
            first_share(0)
            grow_out(1)
            with dve.Fori(1, PAIRS) as q:
                first_share(q)
            for q in range(PAIRS):
                second_share(q, 0)
                if q == 0:
                    sums_out(0)
                    dve.wait_ge(bad_summed, 1)
                    nc.vector.tensor_copy(flag[0:1, :], accs[0:1, 4, 0:1]).then_inc(flag_ready, 1)
                g = q // 2
                if q % 2 == 0 and 0 < g < NB + 1:
                    elu(g - 1)
                if q % 2 == 1 and g < NB:
                    invert(g)
                second_share(q, 1)
                if q % 2 == 1 and 0 < g < NB + 1:
                    statistics(g - 1)
                if q % 2 == 0 and 1 < g < NB + 2:
                    norm(g - 2)
            sums_out(1)
            invert(NB)
            for g in range(NB, GROUPS):
                if g + 1 < GROUPS:
                    invert(g + 1)
                elu(g)
                if g > NB:
                    statistics(g - 1)
            statistics(GROUPS - 1)
            for g in range(NB, GROUPS):
                norm(g)

        @block.tensor
        def _(pe):
            pe.wait_ge(exps_ready, 1)
            for c in range(8):
                for n in range(GROUP):
                    t = c * GROUP + n
                    last = nc.tensor.matmul(accs[:, c, n * P:(n + 1) * P], src[:, t:t + 1].to_broadcast([P, P]),
                                            ident[:, :], start=True, stop=True)
                last.then_inc(spread, 1)

            def aggregate(u, share, at, banks, first, last):
                for c in range(*banks):
                    if first:
                        copied(pe, share, c - FIRST[share], grow_act, grow_dve)
                    ins = nc.tensor.matmul(accs[:, c, :], feats[:, u, :],
                                           ring[:, at + (c - banks[0]) * BANK:at + (c - banks[0] + 1) * BANK],
                                           start=first, stop=last)
                    if last:
                        ins.then_inc(acc_done, 1)
                if not last:
                    ins.then_inc(used, 1)

            def first_share(j, u, first=False, last=False):
                pe.wait_ge(feats_ready, j + 1)
                for c, banks in enumerate(CHUNKS):
                    pe.wait_ge(weights_ready, NC * j + c + 1)
                    aggregate(u, 0, (u * NB + banks[0]) * BANK, banks, first, last)

            def second_share(j):
                pe.wait_ge(feats_ready, TILES + j + 1)
                pe.wait_ge(weights_ready, NC * TILES + j + 1)
                aggregate(2 + j % DEEP, 1, j % DEEP * NB2 * BANK, (NB, NB + NB2), j == 0, j == TILES - 1)

            def project(g):
                share = int(g >= NB)
                if share == 0:
                    for c in range(g if g >= 2 else 2 * g, g + 1 if g >= 2 else 2 * g + 2):
                        copied(pe, 0, c, sums_act, sums_dve)
                else:
                    copied(pe, 1, g - NB, sums_act, sums_dve)
                if g >= 2:
                    pe.wait_ge(z_ready, g - 1)
                for n in range(GROUP):
                    t = GROUP * g + n
                    last = nc.tensor.matmul(slots(g)[:, n, 0:D + 1], sumsT[:, t * P:(t + 1) * P], w_out[:, :],
                                            start=True, stop=True)
                last.then_inc(projected, 1)

            first_share(0, 0, first=True)
            first_share(1, 1)
            with pe.Fori(1, PAIRS - 1) as q:
                first_share(2 * q, 0)
                first_share(2 * q + 1, 1)
            first_share(TILES - 2, 0)
            first_share(TILES - 1, 1, last=True)
            for q in range(PAIRS):
                second_share(2 * q)
                if q == 0:
                    pe.wait_ge(bad_ready, 1)
                    pe.wait_ge(consts_ready, 4)
                    copied(pe, 0, 4, sums_act, sums_dve)
                    nc.tensor.matmul(accs[0:1, 4, 0:1], bad1[:, :], ones[:, :], start=True, stop=True
                                     ).then_inc(bad_summed, 1)
                second_share(2 * q + 1)
                if q % 2 == 0 and q // 2 < NB:
                    project(q // 2)
            for g in range(NB, GROUPS):
                project(g)


def general_layer(nc, ident, flag, x_sb, h_sb, adj, out, w, bias, att_row, b_att, masked, leaky):
    tag = f"general{int(leaky)}_"
    with ExitStack() as ctx:
        sb = lambda name, shape, dt: ctx.enter_context(nc.sbuf_tensor(name, shape, dt))
        sem = lambda name: ctx.enter_context(nc.semaphore(name))
        w_sb, bias_sb, b_att_sb = sb(tag + "w", [P, D], F32), sb(tag + "bias", [P, D], F32), sb(tag + "b_att", [P, 1], F32)
        att_sb = sb(tag + "att", [P, 2, D], F32)
        d_row = sb(tag + "d_row", [P, N], F32)
        logit, mask, adj_t = sb(tag + "logit", [P, N], F32), sb(tag + "mask", [P, N], F32), sb(tag + "adj", [P, N], I32)
        xt, xT, ht = sb(tag + "xt", [P, D], F32), sb(tag + "xT", [P, P], F32), sb(tag + "ht", [P, D], F32)
        prod, sd = sb(tag + "prod", [P, 2, D], F32), sb(tag + "sd", [P, 2], F32)
        s_all = sb(tag + "s", [P, TILES], F32)
        neg_max, total, linv = sb(tag + "neg_max", [P, 1], F32), sb(tag + "total", [P, 1], F32), sb(tag + "linv", [P, 1], F32)
        weightsT = sb(tag + "wT", [P, 2, GROUP * P], F32)
        y, z = sb(tag + "y", [P, D], F32), sb(tag + "z", [P, D], F32)
        mean, var, std = sb(tag + "mean", [P, 1], F32), sb(tag + "var", [P, 1], F32), sb(tag + "std", [P, 1], F32)
        eps = sb(tag + "eps", [P, 1], F32)
        ps = ctx.enter_context(nc.psum_tensor(tag + "ps", [P, 6, BANK], F32))
        x_ps, h_ps, row_ps, sum_ps, turn_ps = ps[:, 0, 0:P], ps[:, 1, 0:D], ps[:, 2, 0:P], ps[:, 3, 0:D], ps[:, 4:6, :]
        (landed, xt_ready, xt_turned, xT_ready, h_done, sd_ready, row_made, row_ready, adj_landed, adj_read,
         max_ready, exp_done, turned, turned_out, summed, low_ready, low_exp, var_ready, std_ready, tile_done, out_done,
         one, two, consts_ready) = (sem(tag + n) for n in (
             "landed", "xt_ready", "xt_turned", "xT_ready", "h_done", "sd_ready", "row_made", "row_ready", "adj_landed",
             "adj_read", "max_ready", "exp_done", "turned", "turned_out", "summed", "low_ready", "low_exp", "var_ready",
             "std_ready", "tile_done", "out_done", "one", "two", "consts_ready"))
        LOADS = 2 + (bias is not None) + (b_att is not None)
        ONE, TWO = 4, 13 + 2 * leaky
        block = ctx.enter_context(nc.Block())

        @block.sync
        def _(sp):
            with sp.If(sp.value_load(flag[0:1, 0:1]) != 0):
                sp.dma_start(w_sb[:, :], w).then_inc(landed, 16)
                sp.dma_start(att_sb[:, :, :].rearrange("p s d -> p (s d)"), att_row.to_broadcast([P, 2 * D])
                             ).then_inc(landed, 16)
                if bias is not None:
                    sp.dma_start(bias_sb[:, :], bias.to_broadcast([P, D])).then_inc(landed, 16)
                if b_att is not None:
                    sp.dma_start(b_att_sb[:, :], b_att.to_broadcast([P, 1])).then_inc(landed, 16)
                sp.dma_start(adj_t[:, :], adj[0]).then_inc(adj_landed, 16)
                with sp.Fori(1, TILES) as t:
                    sp.wait_ge(adj_read, t)
                    sp.dma_start(adj_t[:, :], adj[bass.ds(t, 1)].rearrange("o p j -> p (o j)")).then_inc(adj_landed, 16)
                if out is not None:
                    sp.wait_ge(tile_done, 2 * TILES)
                    sp.dma_start(out.rearrange("(t p) f -> p t f", p=P), x_sb[:, :, :]).then_inc(out_done, 16)
                    sp.wait_ge(out_done, 16)

        @block.gpsimd
        def _(pool):
            with pool.If(pool.value_load(flag[0:1, 0:1]) != 0):
                last = nc.gpsimd.memset(eps[:, :], EPS)
                if bias is None:
                    last = nc.gpsimd.memset(bias_sb[:, :], 0.0)
                if b_att is None:
                    last = nc.gpsimd.memset(b_att_sb[:, :], 0.0)
                last.then_inc(consts_ready, 1)

        @block.scalar
        def _(act):
            with act.If(act.value_load(flag[0:1, 0:1]) != 0):
                act.wait_ge(landed, 16 * LOADS)
                act.wait_ge(consts_ready, 1)
                with act.Fori(0, TILES) as t:
                    act.wait_ge(xt_turned, t + 1)
                    nc.scalar.copy(xT[:, :], x_ps).then_inc(xT_ready, 1)
                    act.wait_ge(row_made, t + 1)
                    nc.scalar.copy(d_row[:, bass.ds(t * P, P)], row_ps).then_inc(row_ready, 1)
                with act.Fori(0, TILES) as t:
                    act.wait_ge(max_ready, t + 1)
                    nc.scalar.activation(logit[:, :], logit[:, :], ACT.Exp, bias=neg_max[:, :]).then_inc(exp_done, 1)
                    for g in range(GROUPS):
                        act.wait_ge(turned, GROUPS * t + g + 1)
                        nc.scalar.copy(weightsT[:, g % 2, :], turn_ps[:, g % 2, :]).then_inc(turned_out, 1)
                    if leaky:
                        act.wait_ge(low_ready, t + 1)
                        nc.scalar.activation(z[:, :], z[:, :], ACT.Exp).then_inc(low_exp, 1)
                    act.wait_ge(var_ready, t + 1)
                    nc.scalar.activation(std[:, :], var[:, :], ACT.Sqrt, bias=eps[:, :], scale=1.0 / D
                                         ).then_inc(std_ready, 1)

        @block.tensor
        def _(pe):
            with pe.If(pe.value_load(flag[0:1, 0:1]) != 0):
                pe.wait_ge(landed, 16 * LOADS)
                with pe.Fori(0, TILES) as t:
                    pe.wait_ge(xt_ready, t + 1)
                    nc.tensor.transpose(x_ps, xt[:, :], ident[:, :]).then_inc(xt_turned, 1)
                    pe.wait_ge(xT_ready, t + 1)
                    nc.tensor.matmul(h_ps, xT[:, :], w_sb[:, :], start=True, stop=True).then_inc(h_done, 1)
                    pe.wait_ge(sd_ready, t + 1)
                    nc.tensor.matmul(row_ps, sd[:, 1:2].to_broadcast([P, P]), ident[:, :], start=True, stop=True
                                     ).then_inc(row_made, 1)
                with pe.Fori(0, TILES) as t:
                    def turn(g):
                        if g == 0:
                            pe.wait_ge(exp_done, t + 1)
                        for n in range(GROUP):
                            j = GROUP * g + n
                            last = nc.tensor.transpose(turn_ps[:, g % 2, n * P:(n + 1) * P], logit[:, j * P:(j + 1) * P],
                                                       ident[:, :])
                        last.then_inc(turned, 1)
                    turn(0)
                    for g in range(GROUPS):
                        if g + 1 < GROUPS:
                            turn(g + 1)
                        pe.wait_ge(turned_out, GROUPS * t + g + 1)
                        for n in range(GROUP):
                            j = GROUP * g + n
                            last = nc.tensor.matmul(sum_ps, weightsT[:, g % 2, n * P:(n + 1) * P], h_sb[:, j, :],
                                                    start=(j == 0), stop=(j == TILES - 1))
                    last.then_inc(summed, 1)

        @block.vector
        def _(dve):
            def links(t, sem_, per_tile):
                n = [0]

                def link(ins):
                    n[0] += 1
                    ins.then_inc(sem_, 1)
                    dve.wait_ge(sem_, per_tile * t + n[0])
                return link

            with dve.If(dve.value_load(flag[0:1, 0:1]) != 0):
                dve.wait_ge(landed, 16 * LOADS)
                dve.wait_ge(consts_ready, 1)
                with dve.Fori(0, TILES) as t:
                    link = links(t, one, ONE)
                    nc.vector.tensor_copy(xt[:, :], x_sb[:, bass.ds(t, 1), :].rearrange("p o f -> p (o f)")
                                          ).then_inc(xt_ready, 1)
                    dve.wait_ge(h_done, t + 1)
                    link(nc.vector.tensor_tensor(ht[:, :], h_ps, bias_sb[:, :], ALU.add))
                    nc.vector.tensor_copy(h_sb[:, bass.ds(t, 1), :].rearrange("p o f -> p (o f)"), ht[:, :])
                    link(nc.vector.tensor_tensor(prod[:, :, :], ht[:, :].rearrange("p (o f) -> p o f", o=1)
                                                 .to_broadcast([P, 2, D]), att_sb[:, :, :], ALU.mult))
                    link(nc.vector.tensor_reduce(sd[:, :], prod[:, :, :], AX.X, ALU.add))
                    link(nc.vector.tensor_scalar(s_all[:, bass.ds(t, 1)], sd[:, 0:1], b_att_sb[:, :], None, ALU.add))
                    nc.vector.tensor_copy(prod[:, 0, 0:1], sd[:, 0:1]).then_inc(sd_ready, 1)
                dve.wait_ge(row_ready, TILES)
                with dve.Fori(0, TILES) as t:
                    link = links(t, two, TWO)
                    dve.wait_ge(adj_landed, 16 * (t + 1))
                    nc.vector.tensor_scalar(mask[:, :], adj_t[:, :], 0.0, None, ALU.is_gt).then_inc(adj_read, 1)
                    link(nc.vector.tensor_scalar(logit[:, :], d_row[:, :], s_all[:, bass.ds(t, 1)], None, ALU.add))
                    if leaky:
                        link(nc.vector.scalar_tensor_tensor(out=logit[:, :], in0=logit[:, :], scalar=0.01,
                                                            in1=logit[:, :], op0=ALU.mult, op1=ALU.max))
                    link(nc.vector.tensor_tensor(logit[:, :], logit[:, :], mask[:, :], ALU.mult))
                    link(nc.vector.tensor_scalar(mask[:, :], mask[:, :], -1.0, masked, ALU.add, ALU.mult))
                    link(nc.vector.tensor_tensor(logit[:, :], logit[:, :], mask[:, :], ALU.add))
                    link(nc.vector.tensor_reduce(total[:, :], logit[:, :], AX.X, ALU.max))
                    nc.vector.tensor_scalar(neg_max[:, :], total[:, :], -1.0, None, ALU.mult).then_inc(max_ready, 1)
                    dve.wait_ge(exp_done, t + 1)
                    link(nc.vector.tensor_reduce(total[:, :], logit[:, :], AX.X, ALU.add))
                    link(nc.vector.reciprocal(linv[:, :], total[:, :]))
                    dve.wait_ge(summed, t + 1)
                    xt_ = x_sb[:, bass.ds(t, 1), :].rearrange("p o f -> p (o f)")
                    if leaky:
                        link(nc.vector.tensor_scalar(y[:, :], sum_ps, linv[:, :], None, ALU.mult))
                        nc.vector.tensor_scalar(z[:, :], y[:, :], 0.0, None, ALU.min).then_inc(low_ready, 1)
                        dve.wait_ge(low_exp, t + 1)
                        link(nc.vector.scalar_tensor_tensor(out=y[:, :], in0=y[:, :], scalar=0.0, in1=z[:, :],
                                                            op0=ALU.max, op1=ALU.add))
                        link(nc.vector.scalar_tensor_tensor(out=y[:, :], in0=y[:, :], scalar=-1.0, in1=xt_,
                                                            op0=ALU.add, op1=ALU.add))
                    else:
                        link(nc.vector.tensor_scalar(z[:, :], sum_ps, linv[:, :], None, ALU.mult))
                        link(nc.vector.tensor_tensor(y[:, :], z[:, :], xt_, ALU.add))
                    link(nc.vector.tensor_reduce(mean[:, :], y[:, :], AX.X, ALU.add))
                    link(nc.vector.tensor_scalar(mean[:, :], mean[:, :], 1.0 / D, None, ALU.mult))
                    link(nc.vector.tensor_scalar(y[:, :], y[:, :], mean[:, :], None, ALU.subtract))
                    link(nc.vector.tensor_tensor(z[:, :], y[:, :], y[:, :], ALU.mult))
                    nc.vector.tensor_reduce(var[:, :], z[:, :], AX.X, ALU.add).then_inc(var_ready, 1)
                    dve.wait_ge(std_ready, t + 1)
                    nc.vector.reciprocal(std[:, :], std[:, :]).then_inc(tile_done, 1)
                    dve.wait_ge(tile_done, 2 * t + 1)
                    nc.vector.tensor_scalar(xt_, y[:, :], std[:, :], None, ALU.mult).then_inc(tile_done, 1)


def general_path(nc, ident, flag, x, adj, w_fc, b_fc, w_att, b_att, w_gat, a_gat, out):
    with ExitStack() as ctx:
        x_sb = ctx.enter_context(nc.sbuf_tensor("g_x", [P, TILES, D], F32))
        h_sb = ctx.enter_context(nc.sbuf_tensor("g_h", [P, TILES, D], F32))
        loaded = ctx.enter_context(nc.semaphore("g_loaded"))
        with nc.Block() as block:
            @block.sync
            def _(sp):
                with sp.If(sp.value_load(flag[0:1, 0:1]) != 0):
                    sp.dma_start(x_sb[:, :, :], x.rearrange("(t p) f -> p t f", p=P)).then_inc(loaded, 16)
                    sp.wait_ge(loaded, 16)
        adj_t = adj.rearrange("(t p) j -> t p j", p=P)
        general_layer(nc, ident, flag, x_sb, h_sb, adj_t, None, w_fc, b_fc.rearrange("(o d) -> o d", o=1),
                      w_att.rearrange("(o d) -> o d", o=1), b_att, 1e9, False)
        general_layer(nc, ident, flag, x_sb, h_sb, adj_t, out, w_gat, None,
                      a_gat.rearrange("d o -> o d"), None, 1e12, True)


def build(nc, x, adj, w_fc, b_fc, w_att, b_att, w_gat, a_gat, out):
    x_rows, adj_rows, out_rows = views(x, adj, out)
    with ExitStack() as last, ExitStack() as ctx:
        keep = {}
        for name, shape, dt in (("ident", [P, P], F32), ("flag", [1, 1], I32)):
            keep[name] = last.enter_context(nc.sbuf_tensor(name, shape, dt))
        for name, shape, dt in (("sd1", [P, TILES, 3], F32),
                                ("lsum", [P, TILES], F32), ("sd0", [P, TILES, 2], F32), ("w_out", [P, D + 1], F32),
                                ("x_sb", [P, TILES, D], F32), ("store", [P, TILES, N], U8)):
            keep[name] = ctx.enter_context(nc.sbuf_tensor(name, shape, dt))
        layer_one(nc, keep, x_rows, adj_rows, w_fc, b_fc, w_att, b_att, w_gat, a_gat)
        layer_two(nc, keep, out_rows)
        ctx.close()
        general_path(nc, keep["ident"], keep["flag"], x, adj, w_fc, b_fc, w_att, b_att, w_gat, a_gat, out)


_INS = ['x', 'adj', 'L0_gnn_W_fc', 'L0_gnn_b_fc', 'L0_gnn_w_att', 'L0_gnn_b_att', 'L1_gnn_W', 'L1_gnn_a']


def kernel(**inputs):
    import numpy as np
    import concourse.bacc as bacc
    from concourse.bass_utils import run_bass_kernel_spmd as run

    nc = bacc.Bacc("TRN2", target_bir_lowering=False, num_devices=1)
    arrays, args = {}, []
    for name in _INS:
        a = np.ascontiguousarray(inputs[name])
        if a.ndim == 0 or name == 'L0_gnn_b_att':
            a = a.reshape(1, 1)
        arrays[f"in_{name}"] = a
        args.append(nc.dram_tensor(f"in_{name}", a.shape, mybir.dt.from_np(a.dtype), kind="ExternalInput").ap())
    out = nc.dram_tensor("out_x", (N, D), F32, kind="ExternalOutput").ap()
    build(nc, *args, out)
    r = run(nc, [arrays], core_ids=[0])
    return r.results[0]["out_x"]
```

```python
from contextlib import ExitStack

import concourse.bass as bass
from concourse import mybir

F32 = mybir.dt.float32
BF16 = mybir.dt.bfloat16
FP8 = mybir.dt.float8e4
U8 = mybir.dt.uint8
U16 = mybir.dt.uint16
I32 = mybir.dt.int32
ALU = mybir.AluOpType
ACT = mybir.ActivationFunctionType
AX = mybir.AxisListType

P = 128
N = 4096
D = 128
TILES = N // P
PAIRS = TILES // 2
EARLY = 3
CHUNKS = 4
CW = N // CHUNKS
PARTS = 3
GROUP = 4
GROUPS = TILES // GROUP
SUMS_BANK = 5
BANK = 512
MASK_BYTE = 64
LIMIT = 30.0
TINY = 1e-30
EMPTY = 1e-20
EPS = 1e-5


def views(x, adj, out):
    return (x.rearrange("(q k b) f -> k q (b f)", k=P, b=2),
            adj.rearrange("(q k b) j -> q b k j", k=P, b=2),
            out.rearrange("(q k b) f -> k q (b f)", k=P, b=2))


def layer_one(nc, keep, x_rows, adj_rows, w_fc, b_fc, w_att, b_att, w_gat, a_gat):
    store, x_sb, sd1, lsum, sd0, w_out, ident, avec, banks = (keep[n] for n in (
        "store", "x_sb", "sd1", "lsum", "sd0", "w_out", "ident", "avec", "banks"))
    with ExitStack() as ctx:
        sb = lambda name, shape, dt: ctx.enter_context(nc.sbuf_tensor(name, shape, dt))
        sem = lambda name: ctx.enter_context(nc.semaphore(name))
        parts = sb("parts", [P, TILES, PARTS, D + 1], BF16)
        adj_sb = sb("adj_sb", [P, CHUNKS, CW], I32)
        mask8 = sb("mask8", [P, 2, N], U8)
        stage = sb("stage", [P, 2, N], U8)
        ident16 = sb("ident16", [P, P], BF16)
        w1sd = sb("w1sd", [P, 2], F32)
        bias_row = sb("bias_row", [P, D], F32)
        dconst = sb("dconst", [P, 2], F32)
        b_att_sb = sb("b_att_sb", [P, 1], F32)
        e_in = sb("e_in", [P, 2, GROUP], F32)
        eps = sb("eps", [P, 1], F32)
        minus_half = sb("minus_half", [P, 1], F32)
        sums = sb("sums", [P, D + 1], F32)
        linv = sb("linv", [P, 1], F32)
        held_l = sb("held_l", [P, 1], F32)
        y = sb("y", [P, D], F32)
        stats = sb("stats", [P, 6], F32)
        mv = sb("mv", [P, 2], F32)
        var = sb("var", [P, 1], F32)
        rstd = sb("rstd", [P, 1], F32)
        prod = sb("prod", [P, 3, D], F32)

        def late(tile, at, shape):
            n = 1
            for m in shape:
                n *= m
            flat = store[:, tile, :].bitcast(F32)[:, at:at + n]
            return flat if len(shape) == 1 else flat.rearrange("p (a c) -> p a c", a=shape[0])

        early = [store[:, 8 + 4 * n:12 + 4 * n, :].rearrange("p t c -> p (t c)").bitcast(I32).rearrange(
            "p (a c) -> p a c", a=CHUNKS) for n in range(EARLY)]

        xT = [late(TILES - 1 - n, 0, [GROUP * P]) for n in range(2)]
        g32 = [late(TILES - 3 - n, 0, [GROUP, D + 1]) for n in range(3)]
        last_rep, att_row, gat_row = late(TILES - 6, 0, [P]), late(TILES - 6, 128, [2, D]), late(TILES - 6, 384, [2, D])
        w0, w1 = late(TILES - 7, 0, [D + 2]), late(TILES - 7, 256, [D])
        w_prod, w_prod1 = late(TILES - 7, 384, [2, D]), late(TILES - 7, 640, [2, D])

        turned = banks[:, 0:4, :].rearrange("p b c -> p (b c)").bitcast(BF16).rearrange(
            "p (s q l) -> p s q l", s=2, q=PAIRS)
        acc = banks[:, SUMS_BANK - 1:SUMS_BANK + 1, :]
        hps = banks[:, 6:8, :]
        h_banks = [hps, turned[:, 1, :, :].rearrange("p q l -> p (q l)").bitcast(F32).rearrange("p (a c) -> p a c", a=2)]
        h_ps = [x[:, :, 0:2 * (D + 2)].rearrange("p a (b c) -> p a b c", b=2) for x in h_banks]
        spare = turned[:, 0, :, :].rearrange("p q l -> p (q l)").bitcast(F32)
        avec_ps, last_ps = spare[:, 0:256], spare[:, 256:384]

        x_landed = [sem(f"x_landed{g}") for g in range(4)]
        w_landed, w1_landed = sem("w_landed"), sem("w1_landed")
        adj_landed = [sem(f"adj_landed{c}") for c in range(CHUNKS)]
        early_landed = [[sem(f"early{n}_landed{c}") for c in range(CHUNKS)] for n in range(EARLY)]
        ident_ready, ident16_ready, consts_ready = sem("ident_ready"), sem("ident16_ready"), sem("consts_ready")
        pool_step = sem("pool_step")
        bias_added = sem("bias_added")
        w0_ready, w1sd_ready, w_made = sem("w0_ready"), sem("w1sd_ready"), sem("w_made")
        prep_step = sem("prep_step")
        x_turned, xT_ready, h_ready, e_in_ready, e_ready = (sem(n) for n in (
            "x_turned", "xT_ready", "h_ready", "e_in_ready", "e_ready"))
        g_ready, hi_ready, rest_ready, mid_ready, parts_ready = (sem(n) for n in (
            "g_ready", "hi_ready", "rest_ready", "mid_ready", "parts_ready"))
        chunk_done, mask_turned, staged, stored, sums_ready = (sem(n) for n in (
            "chunk_done", "mask_turned", "staged", "stored", "sums_ready"))
        acc_drained, tile_step, var_ready, var_step, rstd_ready, w_read = (sem(n) for n in (
            "acc_drained", "tile_step", "var_ready", "var_step", "rstd_ready", "w_read"))
        STEPS = 6

        def load_x(eng, g):
            eng.dma_start(x_sb[:, 8 * g:8 * g + 8, :].rearrange("p (q b) f -> p q (b f)", b=2),
                          x_rows[:, 4 * g:4 * g + 4, :]).then_inc(x_landed[g], 16)

        block = ctx.enter_context(nc.Block())

        @block.sync
        def _(sp):
            load_x(sp, 0)
            sp.wait_ge(w_landed, 16 * 4)
            load_x(sp, 2)
            load_x(sp, 3)

            def load(q, b, landing=None, landed=adj_landed, wait=None):
                for c in range(CHUNKS):
                    if wait is not None:
                        sp.wait_ge(chunk_done, wait + c)
                    sp.dma_start((adj_sb if landing is None else landing)[:, c, :],
                                 adj_rows[q, b, :, c * CW:(c + 1) * CW]).then_inc(landed[c], 16)

            load(0, 0)
            load(0, 1, early[0], early_landed[0])
            load(1, 0, early[1], early_landed[1])
            load(1, 1, early[2], early_landed[2])
            load(2, 0, wait=1)
            load(2, 1, wait=CHUNKS * 4 + 1)
            with sp.Fori(3, PAIRS) as q:
                for b in range(2):
                    load(q, b, wait=CHUNKS * (2 * q + b - 1) + 1)

        @block.gpsimd
        def _(pool):
            nc.gpsimd.memset(ident[:, :], 0.0).then_inc(pool_step, 1)
            pool.wait_ge(pool_step, 1)
            nc.gpsimd.affine_select(out=ident[:, :], in_=ident[:, :], compare_op=ALU.not_equal, fill=1.0,
                                    base=0, pattern=[[-1, P]], channel_multiplier=1).then_inc(ident_ready, 1)
            pool.wait_ge(ident_ready, 1)
            nc.gpsimd.tensor_copy(ident16[:, :], ident[:, :]).then_inc(ident16_ready, 1)
            nc.gpsimd.memset(eps[:, :], EPS).then_inc(consts_ready, 1)
            nc.gpsimd.memset(avec[:, 2, :], 1.0 / D).then_inc(consts_ready, 1)
            nc.gpsimd.memset(minus_half[:, :], -0.5).then_inc(consts_ready, 1)
            for g in range(GROUPS):
                pool.wait_ge(hi_ready, g + 1)
                nc.gpsimd.tensor_tensor(g32[g % 3], g32[g % 3], parts[:, GROUP * g:GROUP * (g + 1), 0, :],
                                        ALU.subtract).then_inc(rest_ready, 1)
            pool.wait_ge(w_landed, 16 * 4)
            pool.wait_ge(x_turned, GROUPS)
            for g in range(GROUPS):
                xg = x_sb[:, GROUP * g:GROUP * (g + 1), :]
                nc.gpsimd.tensor_tensor(xg, xg, bias_row[:, :].rearrange("p (o d) -> p o d", o=1).to_broadcast(
                    [P, GROUP, D]), ALU.add).then_inc(bias_added, 1)

            def root(t):
                pool.wait_ge(var_ready, t + 1)
                nc.gpsimd.tensor_tensor(var[:, :], mv[:, 1:2], eps[:, :], ALU.add).then_inc(var_step, 1)
                pool.wait_ge(var_step, t + 1)
                nc.gpsimd.tensor_tensor(rstd[:, :], var[:, :], minus_half[:, :], ALU.pow).then_inc(rstd_ready, 1)

            with pool.Fori(0, TILES - 1) as t:
                root(t)

        @block.scalar
        def _(act):
            act.dma_start(w0[:, 0:D], w_fc).then_inc(w_landed, 16)
            act.dma_start(att_row.rearrange("p s d -> p (s d)"),
                          w_att.rearrange("(o d) -> o d", o=1).to_broadcast([P, 2 * D])).then_inc(w_landed, 16)
            act.dma_start(bias_row[:, :], b_fc.rearrange("(o d) -> o d", o=1).to_broadcast([P, D])
                          ).then_inc(w_landed, 16)
            act.dma_start(b_att_sb[:, :], b_att.to_broadcast([P, 1])).then_inc(w_landed, 16)
            load_x(act, 1)
            act.dma_start(w1, w_gat).then_inc(w1_landed, 16)
            act.dma_start(gat_row.rearrange("p s d -> p (s d)"), a_gat.rearrange("d o -> o d").to_broadcast([P, 2 * D])
                          ).then_inc(w1_landed, 16)

            def turn_out(g):
                act.wait_ge(x_turned, g + 1)
                if g >= 2:
                    act.wait_ge(h_ready, g - 1)
                nc.scalar.copy(xT[g % 2], acc[:, g % 2, :]).then_inc(xT_ready, 1)

            def exp_logits(g):
                act.wait_ge(e_in_ready, g + 1)
                if g >= 3:
                    act.wait_ge(parts_ready, g - 2)
                nc.scalar.activation(g32[g % 3][:, :, D], e_in[:, g % 2, :], ACT.Exp).then_inc(e_ready, 1)

            def first_part(g):
                act.wait_ge(g_ready, g + 1)
                nc.scalar.copy(parts[:, GROUP * g:GROUP * (g + 1), 0, :], g32[g % 3]).then_inc(hi_ready, 1)

            def middle_part(g):
                act.wait_ge(rest_ready, g + 1)
                nc.scalar.copy(parts[:, GROUP * g:GROUP * (g + 1), 1, :], g32[g % 3]).then_inc(mid_ready, 1)

            def stage_mask(t, s, free):
                act.wait_ge(mask_turned, t + 1)
                if free:
                    act.wait_ge(sums_ready, t - 1)
                nc.scalar.copy(stage[:, s, :].bitcast(U16),
                               turned[:, s].rearrange("p q l -> p (q l)").bitcast(U16)).then_inc(staged, 1)

            def store_mask(t, s):
                nc.scalar.copy(store[:, bass.ds(t, 1), :].rearrange("p t n -> p (t n)").bitcast(U16),
                               turned[:, s].rearrange("p q l -> p (q l)").bitcast(U16)).then_inc(stored, 1)

            def pair(q, first=False, last=False):
                stage_mask(2 * q + 1, 1, not first)
                store_mask(2 * q + 1, 1)
                if not last:
                    stage_mask(2 * q + 2, 0, True)
                    store_mask(2 * q + 2, 0)

            turn_out(0)
            turn_out(1)
            exp_logits(0)
            for g in range(GROUPS):
                if g + 2 < GROUPS:
                    turn_out(g + 2)
                first_part(g)
                if g + 1 < GROUPS:
                    exp_logits(g + 1)
                if g == GROUPS - 3:
                    stage_mask(0, 0, False)
                if g >= 1:
                    middle_part(g - 1)
            middle_part(GROUPS - 1)
            store_mask(0, 0)
            pair(0, first=True)
            with act.Fori(1, PAIRS - 1) as q:
                pair(q)
            pair(PAIRS - 1, last=True)

        @block.vector
        def _(dve):
            steps = [0]

            def link(ins):
                steps[0] += 1
                ins.then_inc(prep_step, 1)
                dve.wait_ge(prep_step, steps[0])

            dve.wait_ge(w_landed, 16 * 4)
            link(nc.vector.tensor_tensor(w_prod, att_row, w0[:, 0:D].rearrange("p (o d) -> p o d", o=1)
                                         .to_broadcast([P, 2, D]), ALU.mult))
            nc.vector.tensor_reduce(w0[:, D:D + 2], w_prod, AX.X, ALU.add).then_inc(w0_ready, 1)
            link(nc.vector.tensor_tensor(att_row, att_row, bias_row[:, :].rearrange("p (o d) -> p o d", o=1)
                                         .to_broadcast([P, 2, D]), ALU.mult))
            link(nc.vector.tensor_reduce(dconst[:, :], att_row, AX.X, ALU.add))
            link(nc.vector.tensor_tensor(dconst[:, 0:1], dconst[:, 0:1], b_att_sb[:, :], ALU.add))

            def convert(t, s, c, free):
                land = adj_sb
                if isinstance(t, int) and 1 <= t <= EARLY:
                    land = early[t - 1]
                    dve.wait_ge(early_landed[t - 1][c], 16)
                elif isinstance(t, int) and t == 0:
                    dve.wait_ge(adj_landed[c], 16)
                else:
                    dve.wait_ge(adj_landed[c], 16 * (t + 1 - EARLY))
                if free and c == 0:
                    dve.wait_ge(mask_turned, t - 1)
                nc.vector.tensor_scalar(mask8[:, s, c * CW:(c + 1) * CW], land[:, c, :], 0.0, float(MASK_BYTE),
                                        ALU.is_gt, ALU.mult).then_inc(chunk_done, 1)

            def logits(g):
                dve.wait_ge(h_ready, g + 1)
                gs = slice(GROUP * g, GROUP * (g + 1))
                link(nc.vector.tensor_tensor(sd0[:, gs, :].rearrange("p (a b) c -> p a b c", b=2), h_ps[g % 2][:, :, :, D:D + 2],
                                             dconst[:, :].rearrange("p (a b c) -> p a b c", a=1, b=1)
                                             .to_broadcast([P, 2, 2, 2]), ALU.add))
                if g >= 2:
                    dve.wait_ge(e_ready, g - 1)
                nc.vector.tensor_scalar(e_in[:, g % 2, :], sd0[:, gs, 1], LIMIT, -LIMIT, ALU.min, ALU.max
                                        ).then_inc(e_in_ready, 1)

            def last_part(g):
                dve.wait_ge(mid_ready, g + 1)
                gs = slice(GROUP * g, GROUP * (g + 1))
                nc.vector.tensor_tensor(parts[:, gs, 2, :], g32[g % 3], parts[:, gs, 1, :], ALU.subtract
                                        ).then_inc(parts_ready, 1)

            def second_weights():
                dve.wait_ge(w1_landed, 32)
                dve.wait_ge(ident_ready, 1)
                nc.vector.tensor_copy(last_rep, ident[:, P - 1:P].to_broadcast([P, P]))
                link(nc.vector.tensor_tensor(w_prod1, gat_row, w1.rearrange("p (o d) -> p o d", o=1)
                                             .to_broadcast([P, 2, D]), ALU.mult))
                nc.vector.tensor_reduce(w1sd[:, :], w_prod1, AX.X, ALU.add).then_inc(w1sd_ready, 1)

            def take_second_weights():
                dve.wait_ge(w_made, 1)
                nc.vector.tensor_copy(avec[:, 0:2, :], avec_ps.rearrange("p (s d) -> p s d", s=2))
                nc.vector.tensor_tensor(w_out[:, 0:D], w1, last_ps, ALU.subtract).then_inc(w_read, 1)
                nc.vector.tensor_copy(w_out[:, D:D + 1], ident[:, P - 1:P]).then_inc(consts_ready, 1)

            second_weights()
            logits(0)
            for g in range(GROUPS):
                dve.wait_ge(e_ready, g + 1)
                gg = g32[g % 3]
                gv = gg.rearrange("p (a b) c -> p a b c", b=2)
                nc.vector.tensor_tensor(gv[:, :, :, 0:D], h_ps[g % 2][:, :, :, 0:D],
                                        gv[:, :, :, D:D + 1].to_broadcast([P, 2, 2, D]), ALU.mult).then_inc(g_ready, 1)
                if g + 1 < GROUPS:
                    logits(g + 1)
                if g == 3:
                    take_second_weights()
                if g >= 2:
                    last_part(g - 2)
                for c in ((), (0,), (1,), (2, 3))[g] if g < 4 else ():
                    convert(0, 0, c, False)
            convert(1, 1, 0, False)
            last_part(GROUPS - 2)
            convert(1, 1, 1, False)
            convert(1, 1, 2, False)
            convert(1, 1, 3, False)
            last_part(GROUPS - 1)

            def finish(t, s, cvt):
                def step(ins):
                    n[0] += 1
                    ins.then_inc(tile_step, 1)

                def stepped():
                    dve.wait_ge(tile_step, STEPS * t + n[0])
                n = [0]
                dve.wait_ge(sums_ready, t + 1)
                nc.vector.tensor_reduce(sums[:, :], acc[:, s, 0:PARTS * (D + 1)].rearrange(
                    "p (c f) -> p f c", c=PARTS), AX.X, ALU.add).then_inc(acc_drained, 1)
                cvt(0)
                dve.wait_ge(acc_drained, t + 1)
                step(nc.vector.tensor_scalar(held_l[:, :], sums[:, D:D + 1], TINY, None, ALU.max))
                cvt(1)
                stepped()
                step(nc.vector.reciprocal(linv[:, :], held_l[:, :]))
                cvt(2)
                stepped()
                xt = x_sb[:, bass.ds(t, 1), :].rearrange("p o f -> p (o f)")
                step(nc.vector.scalar_tensor_tensor(out=y[:, :], in0=sums[:, 0:D], scalar=linv[:, :], in1=xt,
                                                    op0=ALU.mult, op1=ALU.add))
                stepped()
                step(nc.vector.bn_stats(stats[:, :], y[:, :]))
                stepped()
                nc.vector.tensor_copy(lsum[:, bass.ds(t, 1)], held_l[:, :])
                nc.vector.bn_aggr(mv[:, :], stats[:, :]).then_inc(var_ready, 1)
                cvt(3)
                dve.wait_ge(rstd_ready, t + 1)
                step(nc.vector.tensor_scalar(xt, y[:, :], mv[:, 0:1], rstd[:, :], ALU.subtract, ALU.mult))
                stepped()
                step(nc.vector.tensor_tensor(prod[:, :, :], x_sb[:, bass.ds(t, 1), :].to_broadcast([P, 3, D]),
                                             avec[:, :, :], ALU.mult))
                stepped()
                nc.vector.tensor_reduce(sd1[:, bass.ds(t, 1), :].rearrange("p o c -> p (o c)"), prod[:, :, :],
                                        AX.X, ALU.add)

            def pair(q, first=False, last=False):
                if first:
                    for c in range(CHUNKS):
                        convert(2, 0, c, True)
                    dve.wait_ge(bias_added, 1)
                else:
                    finish(2 * q - 1, 1, (lambda c: None) if last else (lambda c: convert(2 * q + 2, 0, c, True)))
                finish(2 * q, 0, (lambda c: None) if last else (lambda c: convert(2 * q + 3, 1, c, True)))

            pair(0, first=True)
            dve.wait_ge(bias_added, GROUPS)
            with dve.Fori(1, PAIRS - 1) as q:
                pair(q)
            pair(PAIRS - 1, last=True)

        @block.tensor
        def _(pe):
            def turn_x(g):
                if g % 2 == 0:
                    pe.wait_ge(x_landed[g // 2], 16)
                if g >= 2:
                    pe.wait_ge(xT_ready, g - 1)
                for n in range(GROUP):
                    last = nc.tensor.transpose(acc[:, g % 2, n * P:(n + 1) * P], x_sb[:, GROUP * g + n, :], ident[:, :])
                last.then_inc(x_turned, 1)

            def turn_mask(t, s, free, ahead=None):
                if free:
                    pe.wait_ge(stored, t - 1)
                for c in range(CHUNKS):
                    pe.wait_ge(chunk_done, CHUNKS * t + c + 1)
                    rows = mask8[:, s, c * CW:(c + 1) * CW].bitcast(BF16)
                    for n in range(PAIRS // CHUNKS):
                        if ahead and c == CHUNKS - 1 and n == PAIRS // CHUNKS - 1:
                            ahead()
                        last = nc.tensor.transpose(turned[:, s, c * (PAIRS // CHUNKS) + n, :],
                                                   rows[:, n * P:(n + 1) * P], ident16[:, :])
                last.then_inc(mask_turned, 1)

            def ready(t, free):
                pe.wait_ge(staged, t + 1)
                if free:
                    pe.wait_ge(acc_drained, t - 1)

            def aggregate(s, tiles=range(TILES), first=False):
                for j in tiles:
                    if first and j % GROUP == 0:
                        pe.wait_ge(parts_ready, j // GROUP + 1)
                    last = nc.tensor.matmul(acc[:, s, 0:PARTS * (D + 1)],
                                            stage[:, s, (j // 2) * 2 * P + j % 2:(j // 2 + 1) * 2 * P:2].bitcast(FP8),
                                            parts[:, j, :, :].rearrange("p c f -> p (c f)"),
                                            start=(j == 0), stop=(j == TILES - 1))
                if j == TILES - 1:
                    last.then_inc(sums_ready, 1)

            def pair(q, first=False, last=False):
                if first:
                    ready(0, False)
                    aggregate(0, range(TILES // 2), True)
                    pe.wait_ge(g_ready, GROUPS)
                    turn_mask(1, 1, False)
                    aggregate(0, range(TILES // 2, TILES), True)
                else:
                    turn_mask(2 * q + 1, 1, True, ahead=lambda: ready(2 * q, True))
                    aggregate(0)
                if last:
                    ready(2 * q + 1, True)
                else:
                    turn_mask(2 * q + 2, 0, True, ahead=lambda: ready(2 * q + 1, not first))
                aggregate(1)

            pe.wait_ge(ident_ready, 1)
            turn_x(0)
            turn_x(1)
            pe.wait_ge(w0_ready, 1)
            for g in range(GROUPS):
                pe.wait_ge(xT_ready, g + 1)
                if g >= 2:
                    pe.wait_ge(g_ready, g - 1)
                for n in range(GROUP):
                    last = nc.tensor.matmul(h_ps[g % 2][:, n // 2, n % 2, :], xT[g % 2][:, n * P:(n + 1) * P], w0,
                                            start=True, stop=True)
                last.then_inc(h_ready, 1)
                if g + 2 < GROUPS:
                    turn_x(g + 2)
                if g == 2:
                    pe.wait_ge(w1sd_ready, 1)
                    for c in range(2):
                        nc.tensor.matmul(avec_ps[:, c * D:(c + 1) * D], w1sd[:, c:c + 1].to_broadcast([P, P]),
                                         ident[:, :], start=True, stop=True)
                    nc.tensor.matmul(last_ps, last_rep, w1, start=True, stop=True).then_inc(w_made, 1)
                if g == GROUPS - 3:
                    pe.wait_ge(ident16_ready, 1)
                    pe.wait_ge(w_read, 1)
                    turn_mask(0, 0, False)
            pair(0, first=True)
            with pe.Fori(1, PAIRS - 1) as q:
                pair(q)
            pair(PAIRS - 1, last=True)


def layer_two(nc, keep, out_rows):
    store, x1, sd1, lsum, sd0, w_out, ident, avec, accs, flag = (keep[n] for n in (
        "store", "x_sb", "sd1", "lsum", "sd0", "w_out", "ident", "avec", "banks", "flag"))
    BANKS = (5, 3)
    FIRST = (0, BANKS[0])
    NB, NB2 = BANKS
    CHUNKS = ((0, 3), (3, NB))
    NC = len(CHUNKS)
    FLAG_BANK = BANKS[0] - 1
    FLAG_PAIR = PAIRS - 3
    FIRST_TILES, LAST_TILES = slice(0, TILES - GROUP), slice(TILES - GROUP, TILES)
    DEEP = 3
    with ExitStack() as ctx:
        sb = lambda name, shape, dt: ctx.enter_context(nc.sbuf_tensor(name, shape, dt))
        sem = lambda name: ctx.enter_context(nc.semaphore(name))
        grow = sb("grow", [P, N], F32)
        ring = sb("ring", [P, 2 * NB * BANK], F32)
        y = sb("y2", [P, TILES, D], F32)
        held = sb("held", [P, TILES, 3], F32)
        fac = sb("fac", [P, TILES], F32)
        low = sb("low", [P, TILES], F32)
        nlow = sb("nlow", [P, TILES], F32)
        minus1 = sb("minus1", [P, 1], F32)
        eps = sb("eps2", [P, TILES], F32)
        minus_half = sb("minus_half2", [P, TILES], F32)
        feats = sb("feats", [P, 2 + DEEP, D], F32)
        bad = sb("bad", [P, 3], F32)
        bad1 = sb("bad1", [P, 1], F32)
        ones = sb("ones", [P, 1], F32)
        linv = sb("linv2", [P, GROUPS, GROUP], F32)
        stats = sb("stats2", [P, TILES, 6], F32)
        mv = sb("mv2", [P, TILES, 2], F32)
        var = sb("var2", [P, TILES], F32)
        rstd = sb("rstd2", [P, TILES], F32)
        sums = sb("sums_last", [P, D + 1], F32)
        y_last = sb("y_last", [P, D], F32)
        linv_last, stats_last, mv_last, var_last, rstd_last = (sb(n, [P, w], F32) for n, w in (
            ("linv_last", 1), ("stats_last", 6), ("mv_last", 2), ("var_last", 1), ("rstd_last", 1)))
        prod = sb("prod_last", [P, 3, D], F32)
        shift = sb("shift", [P, TILES], F32)
        sumsT = grow

        consts_ready, held_ready, low_ready, fac_ready, nlow_ready, bad_ready, bad_step = (sem(n) for n in (
            "consts_ready2", "held_ready", "low_ready", "fac_ready", "nlow_ready", "bad_ready", "bad_step"))
        sums_taken, var_last_ready, var_last_step, rstd_last_ready = (sem(n) for n in (
            "sums_taken", "var_last_ready", "var_last_step", "rstd_last_ready"))
        late_feats_ready = sem("late_feats_ready")
        bad_summed, flag_ready, spread = (sem(n) for n in ("bad_summed", "flag_ready", "spread"))
        grown, sums_act, sums_dve = (sem(n) for n in ("grown", "sums_act", "sums_dve"))
        feats_ready, excess_ready, weights_ready, used = (sem(n) for n in (
            "feats_ready", "excess_ready", "weights_ready", "used"))
        acc_done, projected, linv_ready, exp_ready, elu_ready, y_ready = (sem(n) for n in (
            "acc_done", "projected", "linv_ready", "exp_ready", "elu_ready", "y_ready"))
        chain, var_ready, var_step, rstd_ready, shift_ready, out_act, out_dve, out_done = (sem(n) for n in (
            "chain", "var_ready2", "var_step2", "rstd_ready2", "shift_ready", "out_act", "out_dve", "out_done"))
        block = ctx.enter_context(nc.Block())

        def shared(share, c):
            return c % 2 == 0, (FIRST[share] and (NB + 1) // 2) + c // 2 + 1 if c % 2 == 0 else \
                (FIRST[share] and NB // 2) + c // 2 + 1

        def copied(eng, share, c, by_act, by_dve):
            mine, count = shared(share, c)
            eng.wait_ge(by_act if mine else by_dve, count)

        def slot(g):
            return 2 if g == GROUPS - 1 else g % 2

        def slots(g):
            return accs[:, 2 * slot(g):2 * slot(g) + 2, :].rearrange("p a (b c) -> p (a b) c", b=2)

        def positive(g):
            at = (2 * NB - 1 if g < NB else g - NB) * BANK
            return ring[:, at:at + BANK].rearrange("p (t f) -> p t f", f=D)

        def rows(g):
            return slice(GROUP * g, GROUP * (g + 1))

        @block.gpsimd
        def _(pool):
            nc.gpsimd.memset(minus1[:, :], -1.0).then_inc(consts_ready, 1)
            nc.gpsimd.memset(eps[:, :], EPS).then_inc(consts_ready, 1)
            nc.gpsimd.memset(minus_half[:, :], -0.5).then_inc(consts_ready, 1)
            nc.gpsimd.memset(ones[:, :], 1.0).then_inc(consts_ready, 1)
            pool.wait_ge(consts_ready, 4)
            pool.wait_ge(var_last_ready, 1)
            nc.gpsimd.tensor_tensor(var_last[:, :], mv_last[:, 1:2], eps[:, 0:1], ALU.add).then_inc(var_last_step, 1)
            pool.wait_ge(var_last_step, 1)
            nc.gpsimd.tensor_tensor(rstd_last[:, :], var_last[:, :], minus_half[:, 0:1], ALU.pow
                                    ).then_inc(rstd_last_ready, 1)

            def root(g):
                pool.wait_ge(var_ready, g + 1)
                nc.gpsimd.tensor_tensor(var[:, rows(g)], mv[:, rows(g), 1], eps[:, rows(g)], ALU.add).then_inc(var_step, 1)
                pool.wait_ge(var_step, g + 1)
                nc.gpsimd.tensor_tensor(rstd[:, rows(g)], var[:, rows(g)], minus_half[:, rows(g)], ALU.pow
                                        ).then_inc(rstd_ready, 1)

            def residual(g):
                pool.wait_ge(elu_ready, g + 1)
                nc.gpsimd.tensor_tensor(y[:, rows(g), :], y[:, rows(g), :], x1[:, rows(g), :], ALU.add
                                        ).then_inc(y_ready, 1)

            def features(j):
                u = 2 + j % DEEP
                if j >= DEEP:
                    pool.wait_ge(used, NC * (TILES - 1) + j - DEEP + 1)
                nc.gpsimd.tensor_scalar(feats[:, u, 0:D - 1], x1[:, j, 0:D - 1], low[:, j:j + 1], nlow[:, j:j + 1],
                                        ALU.mult, ALU.add)
                nc.gpsimd.tensor_copy(feats[:, u, D - 1:D], low[:, j:j + 1]).then_inc(late_feats_ready, 1)

            pool.wait_ge(nlow_ready, 2)
            pool.wait_ge(low_ready, 2)
            for q in range(PAIRS):
                g = (q - 3) // 2 if q % 2 == 1 and q >= 3 else GROUPS
                features(2 * q)
                if g < NB:
                    residual(g)
                features(2 * q + 1)
                if g < NB:
                    root(g)
            for g in range(NB + 1, GROUPS - 1):
                residual(g)
            for g in range(NB, GROUPS):
                root(g)

        @block.sync
        def _(sp):
            for g in range(GROUPS):
                sp.wait_ge(out_dve, g + 1)
                if g >= NB:
                    sp.wait_ge(out_act, g - NB + 1)
                sp.dma_start(out_rows[:, 2 * g:2 * g + 2, :],
                             y[:, rows(g), :].rearrange("p (q b) f -> p q (b f)", b=2)).then_inc(out_done, 16)
            sp.wait_ge(out_done, 16 * GROUPS)

        @block.scalar
        def _(act):
            def exps(n, tiles):
                act.wait_ge(held_ready, n + 1)
                nc.scalar.activation(low[:, tiles], held[:, tiles, 1], ACT.Exp, scale=0.01).then_inc(low_ready, 1)
                nc.scalar.activation(fac[:, tiles], held[:, tiles, 1], ACT.Exp, scale=0.99).then_inc(fac_ready, 1)

            def grow_out(b):
                act.wait_ge(spread, b + 1)
                nc.scalar.activation(grow[:, b * BANK:(b + 1) * BANK], accs[:, b, :], ACT.Exp, scale=0.99
                                     ).then_inc(grown, 1)

            def sums_out(share):
                for c in range(0, BANKS[share], 2):
                    b = FIRST[share] + c
                    act.wait_ge(acc_done, b + 1)
                    nc.scalar.copy(sumsT[:, b * BANK:(b + 1) * BANK], accs[:, b, :]).then_inc(sums_act, 1)

            def features(j, u):
                nc.scalar.activation(feats[:, u, 0:D - 1], x1[:, bass.ds(j, 1), 0:D - 1].rearrange("p o f -> p (o f)"),
                                     ACT.Identity, bias=nlow[:, bass.ds(j, 1)], scale=low[:, bass.ds(j, 1)])
                nc.scalar.copy(feats[:, u, D - 1:D], low[:, bass.ds(j, 1)]).then_inc(feats_ready, 1)

            def excess(j, at, banks):
                nc.scalar.activation(ring[:, at:at + (banks[1] - banks[0]) * BANK],
                                     grow[:, banks[0] * BANK:banks[1] * BANK], ACT.Relu,
                                     bias=minus1[:, :], scale=fac[:, bass.ds(j, 1)]).then_inc(excess_ready, 1)

            def first_share(j, u, free=True, between=lambda: None):
                if free:
                    act.wait_ge(used, NC * (j - 2) + 1)
                excess(j, u * NB * BANK, CHUNKS[0])
                if free:
                    act.wait_ge(used, NC * (j - 1))
                features(j, u)
                between()
                excess(j, (u * NB + CHUNKS[1][0]) * BANK, CHUNKS[1])

            def second_share(j):
                u = j % DEEP
                if j == 0:
                    act.wait_ge(used, NC * (TILES - 1))
                elif j < DEEP:
                    act.wait_ge(acc_done, min(NB, (j + 1) * NB2 - NB))
                else:
                    act.wait_ge(used, NC * (TILES - 1) + j - DEEP + 1)
                excess(j, u * NB2 * BANK, (NB, NB + NB2))

            def elu_parts(g):
                act.wait_ge(linv_ready, g + 1)
                if 0 < g < NB:
                    act.wait_ge(elu_ready, g)
                for n in range(GROUP):
                    last = nc.scalar.activation(y[:, GROUP * g + n, :], slots(g)[:, n, 0:D], ACT.Exp,
                                                scale=linv[:, g, n:n + 1])
                for n in range(GROUP):
                    last = nc.scalar.activation(positive(g)[:, n, :], slots(g)[:, n, 0:D], ACT.Relu,
                                                scale=linv[:, g, n:n + 1])
                last.then_inc(exp_ready, 1)

            exps(0, FIRST_TILES)
            act.wait_ge(consts_ready, 4)
            for b in range(CHUNKS[0][1]):
                grow_out(b)
            act.wait_ge(fac_ready, 1)
            act.wait_ge(low_ready, 1)
            act.wait_ge(grown, CHUNKS[0][1])
            act.wait_ge(nlow_ready, 1)

            def rest_of_share():
                for b in range(*CHUNKS[1]):
                    grow_out(b)
                act.wait_ge(grown, NB)

            first_share(0, 0, free=False, between=rest_of_share)
            first_share(1, 1, free=False)
            for b in range(NB, 7):
                grow_out(b)
            exps(1, LAST_TILES)
            grow_out(7)
            act.wait_ge(nlow_ready, 2)
            act.wait_ge(fac_ready, 2)
            act.wait_ge(low_ready, 2)
            with act.Fori(1, PAIRS) as q:
                first_share(2 * q, 0)
                first_share(2 * q + 1, 1)
            act.wait_ge(grown, 8)
            for q in range(PAIRS):
                second_share(2 * q)
                if q % 2 == 0 and 0 < q // 2 < NB + 1:
                    elu_parts(q // 2 - 1)
                second_share(2 * q + 1)
                if q == 0:
                    sums_out(0)
            sums_out(1)
            for g in range(NB, GROUPS):
                elu_parts(g)
            for g in range(NB, GROUPS):
                act.wait_ge(shift_ready, g + 1)
                for t in range(GROUP * g, GROUP * g + GROUP // 2):
                    last = nc.scalar.activation(y[:, t, :], y[:, t, :], ACT.Identity, bias=shift[:, t:t + 1],
                                                scale=rstd[:, t:t + 1])
                last.then_inc(out_act, 1)

        @block.vector
        def _(dve):
            steps = [0]

            def link(ins):
                steps[0] += 1
                ins.then_inc(chain, 1)
                dve.wait_ge(chain, steps[0])

            def hold(tiles):
                nc.vector.tensor_scalar(held[:, tiles, :], sd1[:, tiles, :], LIMIT, -LIMIT, ALU.min, ALU.max
                                        ).then_inc(held_ready, 1)

            def shift_features(n, tiles):
                dve.wait_ge(low_ready, n + 1)
                nc.vector.scalar_tensor_tensor(out=nlow[:, tiles], in0=low[:, tiles], scalar=-1.0, in1=sd1[:, tiles, 2],
                                               op0=ALU.mult, op1=ALU.mult).then_inc(nlow_ready, 1)

            def finish_first_layer():
                t = TILES - 1
                nc.vector.tensor_reduce(sums[:, :], accs[:, SUMS_BANK, 0:PARTS * (D + 1)].rearrange(
                    "p (c f) -> p f c", c=PARTS), AX.X, ALU.add).then_inc(sums_taken, 1)
                dve.wait_ge(sums_taken, 1)
                link(nc.vector.tensor_scalar(lsum[:, t:t + 1], sums[:, D:D + 1], TINY, None, ALU.max))
                link(nc.vector.reciprocal(linv_last[:, :], lsum[:, t:t + 1]))
                link(nc.vector.scalar_tensor_tensor(out=y_last[:, :], in0=sums[:, 0:D], scalar=linv_last[:, :],
                                                    in1=x1[:, t, :], op0=ALU.mult, op1=ALU.add))
                link(nc.vector.bn_stats(stats_last[:, :], y_last[:, :]))
                nc.vector.bn_aggr(mv_last[:, :], stats_last[:, :]).then_inc(var_last_ready, 1)
                shift_features(0, FIRST_TILES)
                dve.wait_ge(rstd_last_ready, 1)
                link(nc.vector.tensor_scalar(x1[:, t, :], y_last[:, :], mv_last[:, 0:1], rstd_last[:, :],
                                             ALU.subtract, ALU.mult))
                link(nc.vector.tensor_tensor(prod[:, :, :], x1[:, t:t + 1, :].to_broadcast([P, 3, D]), avec[:, :, :],
                                             ALU.mult))
                link(nc.vector.tensor_reduce(sd1[:, t, :], prod[:, :, :], AX.X, ALU.add))

            def find_bad():
                nc.vector.tensor_reduce(bad[:, 0:1], sd0[:, :, :], AX.XY, ALU.max, apply_absolute_value=True)
                nc.vector.tensor_reduce(bad[:, 1:2], sd1[:, :, 0:2], AX.XY, ALU.max, apply_absolute_value=True)
                nc.vector.tensor_reduce(bad[:, 2:3], lsum[:, :], AX.X, ALU.min).then_inc(bad_step, 1)
                dve.wait_ge(bad_step, 1)
                nc.vector.tensor_scalar(bad[:, 0:2], bad[:, 0:2], LIMIT, None, ALU.is_gt)
                nc.vector.tensor_scalar(bad[:, 2:3], bad[:, 2:3], EMPTY, None, ALU.is_lt).then_inc(bad_step, 1)
                dve.wait_ge(bad_step, 2)
                nc.vector.tensor_reduce(bad1[:, :], bad[:, :], AX.X, ALU.add).then_inc(bad_ready, 1)

            def sums_out(share):
                for c in range(1, BANKS[share], 2):
                    b = FIRST[share] + c
                    dve.wait_ge(acc_done, b + 1)
                    nc.vector.tensor_copy(sumsT[:, b * BANK:(b + 1) * BANK], accs[:, b, :]).then_inc(sums_dve, 1)

            def weigh(q, u, at, banks, count):
                dve.wait_ge(excess_ready, count)
                r = ring[:, at:at + (banks[1] - banks[0]) * BANK].rearrange("p (t l) -> p t l", l=P)
                m = store[:, banks[0] * GROUP:banks[1] * GROUP, bass.ds(2 * P * q + u, P, 2)]
                nc.vector.scalar_tensor_tensor(out=r, in0=r, scalar=1.0, in1=m, op0=ALU.add, op1=ALU.mult
                                               ).then_inc(weights_ready, 1)

            def first_share(q):
                for u in range(2):
                    for c, banks in enumerate(CHUNKS):
                        weigh(q, u, (u * NB + banks[0]) * BANK, banks, NC * (2 * q + u) + c + 1)

            def second_share(q, u):
                j = 2 * q + u
                weigh(q, u, j % DEEP * NB2 * BANK, (NB, NB + NB2), NC * TILES + j + 1)

            def invert(g):
                dve.wait_ge(projected, g + 1)
                link(nc.vector.tensor_scalar(linv[:, g, :], slots(g)[:, :, D], TINY, None, ALU.max))
                nc.vector.reciprocal(linv[:, g, :], linv[:, g, :]).then_inc(linv_ready, 1)

            def elu(g):
                dve.wait_ge(exp_ready, g + 1)
                nc.vector.scalar_tensor_tensor(out=y[:, rows(g), :], in0=y[:, rows(g), :], scalar=1.0,
                                               in1=positive(g), op0=ALU.min, op1=ALU.add
                                               ).then_inc(elu_ready, 1)

            def add_residual(g):
                dve.wait_ge(elu_ready, g + 1)
                link(nc.vector.tensor_tensor(y[:, rows(g), :], y[:, rows(g), :], x1[:, rows(g), :], ALU.add))

            def statistics(g):
                if g not in (NB, GROUPS - 1):
                    dve.wait_ge(y_ready, g + (g < NB))
                for t in range(GROUP * g, GROUP * (g + 1)):
                    last = nc.vector.bn_stats(stats[:, t, :], y[:, t, :])
                link(last)
                for t in range(GROUP * g, GROUP * (g + 1)):
                    last = nc.vector.bn_aggr(mv[:, t, :], stats[:, t, :])
                last.then_inc(var_ready, 1)

            def norm(g):
                dve.wait_ge(rstd_ready, g + 1)
                nc.vector.scalar_tensor_tensor(out=shift[:, rows(g)], in0=mv[:, rows(g), 0], scalar=-1.0,
                                               in1=rstd[:, rows(g)], op0=ALU.mult, op1=ALU.mult).then_inc(shift_ready, 1)
                dve.wait_ge(shift_ready, g + 1)
                for t in range(GROUP * g + (0 if g < NB else GROUP // 2), GROUP * (g + 1)):
                    last = nc.vector.tensor_scalar(y[:, t, :], y[:, t, :], rstd[:, t:t + 1], shift[:, t:t + 1],
                                                   ALU.mult, ALU.add)
                last.then_inc(out_dve, 1)

            hold(FIRST_TILES)
            finish_first_layer()
            hold(LAST_TILES)
            first_share(0)
            shift_features(1, LAST_TILES)
            find_bad()
            with dve.Fori(1, PAIRS) as q:
                first_share(q)
            for q in range(PAIRS):
                second_share(q, 0)
                g = q // 2
                if q % 2 == 1 and 0 < g < NB + 1:
                    statistics(g - 1)
                if q % 2 == 0 and 1 < g < NB + 2:
                    norm(g - 2)
                second_share(q, 1)
                if q == 0:
                    sums_out(0)
                if q == FLAG_PAIR + 1:
                    dve.wait_ge(bad_summed, 1)
                    nc.vector.tensor_copy(flag[0:1, :], accs[0:1, FLAG_BANK, 0:1]).then_inc(flag_ready, 1)
                if q % 2 == 0 and 0 < g < NB + 1:
                    elu(g - 1)
                if q % 2 == 1 and g < NB:
                    invert(g)
            sums_out(1)
            for g in range(NB, GROUPS):
                invert(g)
            elu(NB)
            add_residual(NB)
            statistics(NB)
            for g in range(NB + 1, GROUPS):
                elu(g)
            add_residual(GROUPS - 1)
            for g in range(NB + 1, GROUPS):
                statistics(g)
            for g in range(NB, GROUPS):
                norm(g)

        @block.tensor
        def _(pe):
            def spread_sources(b):
                for n in range(GROUP):
                    last = nc.tensor.matmul(accs[:, b, n * P:(n + 1) * P],
                                            held[:, b * GROUP + n, 0:1].to_broadcast([P, P]), ident[:, :],
                                            start=True, stop=True)
                last.then_inc(spread, 1)

            def aggregate(u, at, banks, first, last):
                for c in range(*banks):
                    if first:
                        pe.wait_ge(grown, c + 1)
                    ins = nc.tensor.matmul(accs[:, c, :], feats[:, u, :],
                                           ring[:, at + (c - banks[0]) * BANK:at + (c - banks[0] + 1) * BANK],
                                           start=first, stop=last)
                    if last:
                        ins.then_inc(acc_done, 1)
                if not last:
                    ins.then_inc(used, 1)

            def first_share(j, u, first=False, last=False):
                pe.wait_ge(feats_ready, j + 1)
                for c, banks in enumerate(CHUNKS):
                    pe.wait_ge(weights_ready, NC * j + c + 1)
                    aggregate(u, (u * NB + banks[0]) * BANK, banks, first, last)

            def second_share(j):
                pe.wait_ge(late_feats_ready, j + 1)
                pe.wait_ge(weights_ready, NC * TILES + j + 1)
                aggregate(2 + j % DEEP, j % DEEP * NB2 * BANK, (NB, NB + NB2), j == 0, j == TILES - 1)

            def project(g):
                share = int(g >= NB)
                if share == 0:
                    for c in range(g if g >= 2 else 2 * g, g + 1 if g >= 2 else 2 * g + 2):
                        copied(pe, 0, c, sums_act, sums_dve)
                else:
                    copied(pe, 1, g - NB, sums_act, sums_dve)
                if slot(g) == 2:
                    copied(pe, 0, 4, sums_act, sums_dve)
                    copied(pe, 1, 0, sums_act, sums_dve)
                    pe.wait_ge(flag_ready, 1)
                elif g >= 2:
                    pe.wait_ge(exp_ready, g - 1)
                for n in range(GROUP):
                    t = GROUP * g + n
                    last = nc.tensor.matmul(slots(g)[:, n, 0:D + 1], sumsT[:, t * P:(t + 1) * P], w_out[:, :],
                                            start=True, stop=True)
                last.then_inc(projected, 1)

            pe.wait_ge(held_ready, 1)
            for b in range(7):
                if b == SUMS_BANK:
                    pe.wait_ge(sums_taken, 1)
                spread_sources(b)
            pe.wait_ge(held_ready, 2)
            spread_sources(7)
            first_share(0, 0, first=True)
            first_share(1, 1)
            with pe.Fori(1, PAIRS - 1) as q:
                first_share(2 * q, 0)
                first_share(2 * q + 1, 1)
            first_share(TILES - 2, 0)
            first_share(TILES - 1, 1, last=True)
            for q in range(PAIRS):
                second_share(2 * q)
                if q == FLAG_PAIR:
                    pe.wait_ge(bad_ready, 1)
                    pe.wait_ge(consts_ready, 4)
                    copied(pe, 0, FLAG_BANK, sums_act, sums_dve)
                    nc.tensor.matmul(accs[0:1, FLAG_BANK, 0:1], bad1[:, :], ones[:, :], start=True, stop=True
                                     ).then_inc(bad_summed, 1)
                second_share(2 * q + 1)
                if q % 2 == 0 and q // 2 < NB:
                    project(q // 2)
            for g in range(NB, GROUPS):
                project(g)


def general_layer(nc, ident, flag, x, x_sb, h_sb, adj, out, w, bias, att_row, b_att, masked, leaky):
    tag = f"general{int(leaky)}_"
    with ExitStack() as ctx:
        sb = lambda name, shape, dt: ctx.enter_context(nc.sbuf_tensor(name, shape, dt))
        sem = lambda name: ctx.enter_context(nc.semaphore(name))
        w_sb, bias_sb, b_att_sb = sb(tag + "w", [P, D], F32), sb(tag + "bias", [P, D], F32), sb(tag + "b_att", [P, 1], F32)
        att_sb = sb(tag + "att", [P, 2, D], F32)
        d_row = sb(tag + "d_row", [P, N], F32)
        logit, mask, adj_t = sb(tag + "logit", [P, N], F32), sb(tag + "mask", [P, N], F32), sb(tag + "adj", [P, N], I32)
        xt, xT, ht = sb(tag + "xt", [P, D], F32), sb(tag + "xT", [P, P], F32), sb(tag + "ht", [P, D], F32)
        prod, sd = sb(tag + "prod", [P, 2, D], F32), sb(tag + "sd", [P, 2], F32)
        s_all = sb(tag + "s", [P, TILES], F32)
        neg_max, total, linv = sb(tag + "neg_max", [P, 1], F32), sb(tag + "total", [P, 1], F32), sb(tag + "linv", [P, 1], F32)
        weightsT = sb(tag + "wT", [P, 2, GROUP * P], F32)
        y, z = sb(tag + "y", [P, D], F32), sb(tag + "z", [P, D], F32)
        mean, var, std = sb(tag + "mean", [P, 1], F32), sb(tag + "var", [P, 1], F32), sb(tag + "std", [P, 1], F32)
        eps = sb(tag + "eps", [P, 1], F32)
        ps = ctx.enter_context(nc.psum_tensor(tag + "ps", [P, 6, BANK], F32))
        x_ps, h_ps, row_ps, sum_ps, turn_ps = ps[:, 0, 0:P], ps[:, 1, 0:D], ps[:, 2, 0:P], ps[:, 3, 0:D], ps[:, 4:6, :]
        (landed, xt_ready, xt_turned, xT_ready, h_done, sd_ready, row_made, row_ready, adj_landed, adj_read,
         max_ready, exp_done, turned, turned_out, summed, low_ready, low_exp, var_ready, std_ready, tile_done, out_done,
         one, two, consts_ready) = (sem(tag + n) for n in (
             "landed", "xt_ready", "xt_turned", "xT_ready", "h_done", "sd_ready", "row_made", "row_ready", "adj_landed",
             "adj_read", "max_ready", "exp_done", "turned", "turned_out", "summed", "low_ready", "low_exp", "var_ready",
             "std_ready", "tile_done", "out_done", "one", "two", "consts_ready"))
        LOADS = 2 + (x is not None) + (bias is not None) + (b_att is not None)
        ONE, TWO = 4, 13 + 2 * leaky
        block = ctx.enter_context(nc.Block())

        @block.sync
        def _(sp):
            with sp.If(sp.value_load(flag[0:1, 0:1]) != 0):
                if x is not None:
                    sp.dma_start(x_sb[:, :, :], x.rearrange("(t p) f -> p t f", p=P)).then_inc(landed, 16)
                sp.dma_start(w_sb[:, :], w).then_inc(landed, 16)
                sp.dma_start(att_sb[:, :, :].rearrange("p s d -> p (s d)"), att_row.to_broadcast([P, 2 * D])
                             ).then_inc(landed, 16)
                if bias is not None:
                    sp.dma_start(bias_sb[:, :], bias.to_broadcast([P, D])).then_inc(landed, 16)
                if b_att is not None:
                    sp.dma_start(b_att_sb[:, :], b_att.to_broadcast([P, 1])).then_inc(landed, 16)
                sp.dma_start(adj_t[:, :], adj[0]).then_inc(adj_landed, 16)
                with sp.Fori(1, TILES) as t:
                    sp.wait_ge(adj_read, t)
                    sp.dma_start(adj_t[:, :], adj[bass.ds(t, 1)].rearrange("o p j -> p (o j)")).then_inc(adj_landed, 16)
                if out is not None:
                    sp.wait_ge(tile_done, 2 * TILES)
                    sp.dma_start(out.rearrange("(t p) f -> p t f", p=P), x_sb[:, :, :]).then_inc(out_done, 16)
                    sp.wait_ge(out_done, 16)

        @block.gpsimd
        def _(pool):
            with pool.If(pool.value_load(flag[0:1, 0:1]) != 0):
                last = nc.gpsimd.memset(eps[:, :], EPS)
                if bias is None:
                    last = nc.gpsimd.memset(bias_sb[:, :], 0.0)
                if b_att is None:
                    last = nc.gpsimd.memset(b_att_sb[:, :], 0.0)
                last.then_inc(consts_ready, 1)

        @block.scalar
        def _(act):
            with act.If(act.value_load(flag[0:1, 0:1]) != 0):
                act.wait_ge(landed, 16 * LOADS)
                act.wait_ge(consts_ready, 1)
                with act.Fori(0, TILES) as t:
                    act.wait_ge(xt_turned, t + 1)
                    nc.scalar.copy(xT[:, :], x_ps).then_inc(xT_ready, 1)
                    act.wait_ge(row_made, t + 1)
                    nc.scalar.copy(d_row[:, bass.ds(t * P, P)], row_ps).then_inc(row_ready, 1)
                with act.Fori(0, TILES) as t:
                    act.wait_ge(max_ready, t + 1)
                    nc.scalar.activation(logit[:, :], logit[:, :], ACT.Exp, bias=neg_max[:, :]).then_inc(exp_done, 1)
                    for g in range(GROUPS):
                        act.wait_ge(turned, GROUPS * t + g + 1)
                        nc.scalar.copy(weightsT[:, g % 2, :], turn_ps[:, g % 2, :]).then_inc(turned_out, 1)
                    if leaky:
                        act.wait_ge(low_ready, t + 1)
                        nc.scalar.activation(z[:, :], z[:, :], ACT.Exp).then_inc(low_exp, 1)
                    act.wait_ge(var_ready, t + 1)
                    nc.scalar.activation(std[:, :], var[:, :], ACT.Sqrt, bias=eps[:, :], scale=1.0 / D
                                         ).then_inc(std_ready, 1)

        @block.tensor
        def _(pe):
            with pe.If(pe.value_load(flag[0:1, 0:1]) != 0):
                pe.wait_ge(landed, 16 * LOADS)
                with pe.Fori(0, TILES) as t:
                    pe.wait_ge(xt_ready, t + 1)
                    nc.tensor.transpose(x_ps, xt[:, :], ident[:, :]).then_inc(xt_turned, 1)
                    pe.wait_ge(xT_ready, t + 1)
                    nc.tensor.matmul(h_ps, xT[:, :], w_sb[:, :], start=True, stop=True).then_inc(h_done, 1)
                    pe.wait_ge(sd_ready, t + 1)
                    nc.tensor.matmul(row_ps, sd[:, 1:2].to_broadcast([P, P]), ident[:, :], start=True, stop=True
                                     ).then_inc(row_made, 1)
                with pe.Fori(0, TILES) as t:
                    def turn(g):
                        if g == 0:
                            pe.wait_ge(exp_done, t + 1)
                        for n in range(GROUP):
                            j = GROUP * g + n
                            last = nc.tensor.transpose(turn_ps[:, g % 2, n * P:(n + 1) * P], logit[:, j * P:(j + 1) * P],
                                                       ident[:, :])
                        last.then_inc(turned, 1)
                    turn(0)
                    for g in range(GROUPS):
                        if g + 1 < GROUPS:
                            turn(g + 1)
                        pe.wait_ge(turned_out, GROUPS * t + g + 1)
                        for n in range(GROUP):
                            j = GROUP * g + n
                            last = nc.tensor.matmul(sum_ps, weightsT[:, g % 2, n * P:(n + 1) * P], h_sb[:, j, :],
                                                    start=(j == 0), stop=(j == TILES - 1))
                    last.then_inc(summed, 1)

        @block.vector
        def _(dve):
            def links(t, sem_, per_tile):
                n = [0]

                def link(ins):
                    n[0] += 1
                    ins.then_inc(sem_, 1)
                    dve.wait_ge(sem_, per_tile * t + n[0])
                return link

            with dve.If(dve.value_load(flag[0:1, 0:1]) != 0):
                dve.wait_ge(landed, 16 * LOADS)
                dve.wait_ge(consts_ready, 1)
                with dve.Fori(0, TILES) as t:
                    link = links(t, one, ONE)
                    nc.vector.tensor_copy(xt[:, :], x_sb[:, bass.ds(t, 1), :].rearrange("p o f -> p (o f)")
                                          ).then_inc(xt_ready, 1)
                    dve.wait_ge(h_done, t + 1)
                    link(nc.vector.tensor_tensor(ht[:, :], h_ps, bias_sb[:, :], ALU.add))
                    nc.vector.tensor_copy(h_sb[:, bass.ds(t, 1), :].rearrange("p o f -> p (o f)"), ht[:, :])
                    link(nc.vector.tensor_tensor(prod[:, :, :], ht[:, :].rearrange("p (o f) -> p o f", o=1)
                                                 .to_broadcast([P, 2, D]), att_sb[:, :, :], ALU.mult))
                    link(nc.vector.tensor_reduce(sd[:, :], prod[:, :, :], AX.X, ALU.add))
                    link(nc.vector.tensor_scalar(s_all[:, bass.ds(t, 1)], sd[:, 0:1], b_att_sb[:, :], None, ALU.add))
                    nc.vector.tensor_copy(prod[:, 0, 0:1], sd[:, 0:1]).then_inc(sd_ready, 1)
                dve.wait_ge(row_ready, TILES)
                with dve.Fori(0, TILES) as t:
                    link = links(t, two, TWO)
                    dve.wait_ge(adj_landed, 16 * (t + 1))
                    nc.vector.tensor_scalar(mask[:, :], adj_t[:, :], 0.0, None, ALU.is_gt).then_inc(adj_read, 1)
                    link(nc.vector.tensor_scalar(logit[:, :], d_row[:, :], s_all[:, bass.ds(t, 1)], None, ALU.add))
                    if leaky:
                        link(nc.vector.scalar_tensor_tensor(out=logit[:, :], in0=logit[:, :], scalar=0.01,
                                                            in1=logit[:, :], op0=ALU.mult, op1=ALU.max))
                    link(nc.vector.tensor_tensor(logit[:, :], logit[:, :], mask[:, :], ALU.mult))
                    link(nc.vector.tensor_scalar(mask[:, :], mask[:, :], -1.0, masked, ALU.add, ALU.mult))
                    link(nc.vector.tensor_tensor(logit[:, :], logit[:, :], mask[:, :], ALU.add))
                    link(nc.vector.tensor_reduce(total[:, :], logit[:, :], AX.X, ALU.max))
                    nc.vector.tensor_scalar(neg_max[:, :], total[:, :], -1.0, None, ALU.mult).then_inc(max_ready, 1)
                    dve.wait_ge(exp_done, t + 1)
                    link(nc.vector.tensor_reduce(total[:, :], logit[:, :], AX.X, ALU.add))
                    link(nc.vector.reciprocal(linv[:, :], total[:, :]))
                    dve.wait_ge(summed, t + 1)
                    xt_ = x_sb[:, bass.ds(t, 1), :].rearrange("p o f -> p (o f)")
                    if leaky:
                        link(nc.vector.tensor_scalar(y[:, :], sum_ps, linv[:, :], None, ALU.mult))
                        nc.vector.tensor_scalar(z[:, :], y[:, :], 0.0, None, ALU.min).then_inc(low_ready, 1)
                        dve.wait_ge(low_exp, t + 1)
                        link(nc.vector.scalar_tensor_tensor(out=y[:, :], in0=y[:, :], scalar=0.0, in1=z[:, :],
                                                            op0=ALU.max, op1=ALU.add))
                        link(nc.vector.scalar_tensor_tensor(out=y[:, :], in0=y[:, :], scalar=-1.0, in1=xt_,
                                                            op0=ALU.add, op1=ALU.add))
                    else:
                        link(nc.vector.tensor_scalar(z[:, :], sum_ps, linv[:, :], None, ALU.mult))
                        link(nc.vector.tensor_tensor(y[:, :], z[:, :], xt_, ALU.add))
                    link(nc.vector.tensor_reduce(mean[:, :], y[:, :], AX.X, ALU.add))
                    link(nc.vector.tensor_scalar(mean[:, :], mean[:, :], 1.0 / D, None, ALU.mult))
                    link(nc.vector.tensor_scalar(y[:, :], y[:, :], mean[:, :], None, ALU.subtract))
                    link(nc.vector.tensor_tensor(z[:, :], y[:, :], y[:, :], ALU.mult))
                    nc.vector.tensor_reduce(var[:, :], z[:, :], AX.X, ALU.add).then_inc(var_ready, 1)
                    dve.wait_ge(std_ready, t + 1)
                    nc.vector.reciprocal(std[:, :], std[:, :]).then_inc(tile_done, 1)
                    dve.wait_ge(tile_done, 2 * t + 1)
                    nc.vector.tensor_scalar(xt_, y[:, :], std[:, :], None, ALU.mult).then_inc(tile_done, 1)


def general_path(nc, ident, flag, x, adj, w_fc, b_fc, w_att, b_att, w_gat, a_gat, out):
    with ExitStack() as ctx:
        x_sb = ctx.enter_context(nc.sbuf_tensor("g_x", [P, TILES, D], F32))
        h_sb = ctx.enter_context(nc.sbuf_tensor("g_h", [P, TILES, D], F32))
        adj_t = adj.rearrange("(t p) j -> t p j", p=P)
        general_layer(nc, ident, flag, x, x_sb, h_sb, adj_t, None, w_fc, b_fc.rearrange("(o d) -> o d", o=1),
                      w_att.rearrange("(o d) -> o d", o=1), b_att, 1e9, False)
        general_layer(nc, ident, flag, None, x_sb, h_sb, adj_t, out, w_gat, None,
                      a_gat.rearrange("d o -> o d"), None, 1e12, True)


def build(nc, x, adj, w_fc, b_fc, w_att, b_att, w_gat, a_gat, out):
    x_rows, adj_rows, out_rows = views(x, adj, out)
    with ExitStack() as last, ExitStack() as ctx:
        keep = {"banks": ctx.enter_context(nc.psum_tensor("banks", [P, 8, BANK], F32))}
        for name, shape, dt in (("ident", [P, P], F32), ("flag", [1, 1], I32)):
            keep[name] = last.enter_context(nc.sbuf_tensor(name, shape, dt))
        for name, shape, dt in (("sd1", [P, TILES, 3], F32),
                                ("lsum", [P, TILES], F32), ("sd0", [P, TILES, 2], F32), ("w_out", [P, D + 1], F32),
                                ("avec", [P, 3, D], F32),
                                ("x_sb", [P, TILES, D], F32), ("store", [P, TILES, N], U8)):
            keep[name] = ctx.enter_context(nc.sbuf_tensor(name, shape, dt))
        layer_one(nc, keep, x_rows, adj_rows, w_fc, b_fc, w_att, b_att, w_gat, a_gat)
        layer_two(nc, keep, out_rows)
        ctx.close()
        general_path(nc, keep["ident"], keep["flag"], x, adj, w_fc, b_fc, w_att, b_att, w_gat, a_gat, out)


_INS = ['x', 'adj', 'L0_gnn_W_fc', 'L0_gnn_b_fc', 'L0_gnn_w_att', 'L0_gnn_b_att', 'L1_gnn_W', 'L1_gnn_a']


def kernel(**inputs):
    import numpy as np
    import concourse.bacc as bacc
    from concourse.bass_utils import run_bass_kernel_spmd as run

    nc = bacc.Bacc("TRN2", target_bir_lowering=False, num_devices=1)
    arrays, args = {}, []
    for name in _INS:
        a = np.ascontiguousarray(inputs[name])
        if a.ndim == 0 or name == 'L0_gnn_b_att':
            a = a.reshape(1, 1)
        arrays[f"in_{name}"] = a
        args.append(nc.dram_tensor(f"in_{name}", a.shape, mybir.dt.from_np(a.dtype), kind="ExternalInput").ap())
    out = nc.dram_tensor("out_x", (N, D), F32, kind="ExternalOutput").ap()
    build(nc, *args, out)
    r = run(nc, [arrays], core_ids=[0])
    return r.results[0]["out_x"]
```
